# Optimizing a Trainium2 kernel written in Bass

```python
import numpy as np
import jax
import jax.numpy as jnp

def _softmax(x, axis=-1):
    return jax.nn.softmax(x, axis=axis)

def _gelu(x):
    return jax.nn.gelu(x, approximate=True)

def _silu(x):
    return jax.nn.silu(x)

def _sigmoid(x):
    return jax.nn.sigmoid(x)

def _layernorm(x, axis=-1, eps=1e-05):
    m = jnp.mean(x, axis=axis, keepdims=True)
    v = jnp.var(x, axis=axis, keepdims=True)
    return (x - m) / jnp.sqrt(v + eps)

def _scatter_add(tgt, idx, src, axis=0):
    return tgt.at[idx].add(src)

def _segment_sum(src, seg, n):
    return jax.ops.segment_sum(src, seg, n)
kernel_name = 'mk_adj_ffn_d1_adj_r2_e00a68'

def setup_inputs(seed: int=0):
    np.random.seed(seed)
    _w = jnp.asarray

    def _rec_inputs():
        import jax
        import jax.numpy as jnp
        _gk = jax.random.key(seed)
        x = -8.776e-05 + 1 * jax.random.normal(jax.random.fold_in(_gk, 1), (10000, 128), jnp.float32)
        _w = (1.0 + jnp.arange(10000, dtype=jnp.float32)) ** (-0.5)
        _w = _w / _w.mean()
        _pij = jnp.clip(0.0008 * _w[:, None] * _w[None, :], 0.0, 1.0)
        _a = jax.random.uniform(jax.random.fold_in(_gk, 2), (10000, 10000)) < _pij
        _a = jnp.logical_or(_a, jnp.eye(10000, dtype=bool))
        _af = _a.astype(jnp.float32)
        _af = _af * jax.random.uniform(jax.random.fold_in(_gk, 3), (10000, 10000), jnp.float32, 0.05, 1)
        adj = _af
        return (x, adj)
    x, adj = _rec_inputs()

    def _L0_gnn_setup():
        import jax, jax.numpy as jnp
        import numpy as np
        N_USER = 10000
        N_ITEM = 10000
        HID = 128
        key = jax.random.key(seed)
        k1, k2, k3, k4, k5, k6, k7 = jax.random.split(key, 7)
        scale = 1.0 / np.sqrt(HID)
        return {'user_feat': jax.random.normal(k1, (N_USER, HID), dtype=jnp.float32), 'item_feat': jax.random.normal(k2, (N_ITEM, HID), dtype=jnp.float32), 'adj': jax.random.uniform(k3, (N_USER, N_ITEM), dtype=jnp.float32), 'W_item': jax.random.uniform(k4, (HID, HID), dtype=jnp.float32, minval=-scale, maxval=scale), 'b_item': jax.random.uniform(k5, (HID,), dtype=jnp.float32, minval=-scale, maxval=scale), 'W_user': jax.random.uniform(k6, (HID, HID), dtype=jnp.float32, minval=-scale, maxval=scale), 'b_user': jax.random.uniform(k7, (HID,), dtype=jnp.float32, minval=-scale, maxval=scale)}
    _L0_gnn_all = _L0_gnn_setup()
    _L0_gnn_in = {k: v for k, v in _L0_gnn_all.items() if k in ('item_feat', 'W_item', 'b_item', 'W_user', 'b_user')}
    del _L0_gnn_all

    def _L0_ffn_setup():
        import math
        import jax, jax.numpy as jnp
        import numpy as np
        CAPACITY_FACTOR = 1.25
        key = jax.random.key(seed)
        ks = jax.random.split(key, 5)
        B, L, D, F, E = (8, 4096, 128, 512, 8)
        h = jax.random.normal(ks[0], (B, L, D), dtype=jnp.float32)
        gate_w = jax.random.normal(ks[1], (D, E), dtype=jnp.float32) * 0.02
        gate_b = jnp.zeros((E,), dtype=jnp.float32)
        w1 = jax.random.normal(ks[2], (E, D, F), dtype=jnp.float32) * (1.0 / math.sqrt(D))
        b1 = jnp.zeros((E, F), dtype=jnp.float32)
        w2 = jax.random.normal(ks[3], (E, F, D), dtype=jnp.float32) * (1.0 / math.sqrt(F))
        b2 = jnp.zeros((E, D), dtype=jnp.float32)
        return {'h': h, 'gate_w': gate_w, 'gate_b': gate_b, 'w1': w1, 'b1': b1, 'w2': w2, 'b2': b2}
    _L0_ffn_all = _L0_ffn_setup()
    _L0_ffn_in = {k: v for k, v in _L0_ffn_all.items() if k in ('gate_w', 'gate_b', 'w1', 'b1', 'w2', 'b2')}
    del _L0_ffn_all
    return {'x': x, 'adj': adj, 'L0_gnn_item_feat': _L0_gnn_in['item_feat'], 'L0_gnn_W_item': _L0_gnn_in['W_item'], 'L0_gnn_b_item': _L0_gnn_in['b_item'], 'L0_gnn_W_user': _L0_gnn_in['W_user'], 'L0_gnn_b_user': _L0_gnn_in['b_user'], 'L0_ffn_gate_w': _L0_ffn_in['gate_w'], 'L0_ffn_gate_b': _L0_ffn_in['gate_b'], 'L0_ffn_w1': _L0_ffn_in['w1'], 'L0_ffn_b1': _L0_ffn_in['b1'], 'L0_ffn_w2': _L0_ffn_in['w2'], 'L0_ffn_b2': _L0_ffn_in['b2']}

def reference(x, adj, L0_gnn_item_feat, L0_gnn_W_item, L0_gnn_b_item, L0_gnn_W_user, L0_gnn_b_user, L0_ffn_gate_w, L0_ffn_gate_b, L0_ffn_w1, L0_ffn_b1, L0_ffn_w2, L0_ffn_b2):
    import jax
    import jax.numpy as jnp

    def _L0_gnn_ref(user_feat, item_feat, adj, W_item, b_item, W_user, b_user):
        import jax, jax.numpy as jnp
        import numpy as np
        N_USER = 10000
        N_ITEM = 10000
        HID = 128
        h = item_feat @ W_item.T + b_item
        b = user_feat @ W_user.T + b_user
        return jax.nn.relu(adj @ h + b)

    def _L0_ffn_ref(h, gate_w, gate_b, w1, b1, w2, b2):
        import math
        import jax, jax.numpy as jnp
        import numpy as np
        CAPACITY_FACTOR = 1.25
        B, L, D = h.shape
        E = gate_w.shape[1]
        T = B * L
        C = max(1, math.ceil(CAPACITY_FACTOR * T / E))
        x = h.reshape(T, D)
        logits = x @ gate_w + gate_b
        probs = jax.nn.softmax(logits, axis=-1)
        idx = jnp.argmax(probs, axis=-1)
        prb = jnp.take_along_axis(probs, idx[:, None], axis=1)[:, 0]
        one_hot = jax.nn.one_hot(idx, E, dtype=jnp.float32)
        pos = (jnp.cumsum(one_hot, axis=0) * one_hot).sum(-1).astype(jnp.int32) - 1
        kept = pos < C
        pos_safe = jnp.where(kept, pos, C)
        buf = jnp.zeros((E, C, D), dtype=h.dtype).at[idx, pos_safe].set(x, mode='drop')
        hmid = jax.nn.relu(jnp.einsum('ecd,edf->ecf', buf, w1) + b1[:, None, :])
        ybuf = jnp.einsum('ecf,efd->ecd', hmid, w2) + b2[:, None, :]
        pos_g = jnp.minimum(pos, C - 1)
        y_tok = ybuf[idx, pos_g] * (prb * kept)[:, None]
        y = y_tok.reshape(B, L, D)
        y = jnp.nan_to_num(y, nan=0.0, posinf=10000.0, neginf=-10000.0)
        return y
    x = x + _L0_gnn_ref(_layernorm(x, axis=-1), L0_gnn_item_feat, adj, L0_gnn_W_item, L0_gnn_b_item, L0_gnn_W_user, L0_gnn_b_user)
    x = x + _L0_ffn_ref(_layernorm(x, axis=-1)[None], L0_ffn_gate_w, L0_ffn_gate_b, L0_ffn_w1, L0_ffn_b1, L0_ffn_w2, L0_ffn_b2)[0]
    return x

_drawn_inputs = setup_inputs


def setup_inputs(seed=0):
    import zlib

    import numpy as np

    out = dict(_drawn_inputs(seed))
    spreads = {'L0_ffn_gate_b': (0.0, 0.1), 'L0_ffn_b1': (0.0, 0.8), 'L0_ffn_b2': (0.0, 0.701)}
    factors = {}
    for name, (base, spread) in spreads.items():
        noise = np.random.default_rng([zlib.crc32(name.encode()), seed]).standard_normal(out[name].shape)
        drawn = base * np.exp(spread * noise) if base else spread * noise
        out[name] = jnp.asarray(drawn.astype(out[name].dtype))
    for name, factor in factors.items():
        out[name] = (out[name] * factor).astype(out[name].dtype)
    return out
```

```python
import concourse.bass as bass
from concourse import mybir
from contextlib import ExitStack

P = 128
T = 10000
N = 10000
D = 128
E = 8
F = 512
FC = F // P
C = 1563
EPS = 1e-5

U = 500
NB = T // U
TP = 125
TJ = U // TP
KT = N // P
REST = N - KT * P
CHUNKS = [3, 3, 3, 4] * 6
NC_ = len(CHUNKS)
FIRST = [sum(CHUNKS[:c]) for c in range(NC_)]
PER_ROW = 13
RAW = 4
SPLIT = 3

ROWS = 112
BLOCKS = 14
CP = ROWS * BLOCKS
GROUPS = [4, 4, 3, 3]
GFIRST = [0, 4, 8, 11]
G = len(GROUPS)
W = 132
MEAN, RSTD, PROB, TOKEN = 128, 129, 130, 131
NOWHERE = 1 << 20

IDENT, TRI, ONES, REV, EOFF, TOK0, CONST_W = 0, 128, 256, 384, 416, 448, 452
WIT, WUT, BITEM, ITREST, GATEW, GATEB, BUSER, B1, B2, WEIGHT_W = 0, 128, 256, 384, 400, 408, 440, 441, 473, 481


def build(nc, adj_main, adj_rest, x, item_t, const, weights, w1, w2, out):
    f32, f32r, i32 = mybir.dt.float32, mybir.dt.float32r, mybir.dt.int32
    ALU, ACT, AX = mybir.AluOpType, mybir.ActivationFunctionType, mybir.AxisListType.X

    slots = nc.dram_tensor("slots", (E * CP, W), f32, kind="Internal").ap()
    x_v = x.rearrange("(u p j) d -> u p j d", p=TP, j=TJ)
    out_v = out.rearrange("(u p j) d -> u p j d", p=TP, j=TJ)
    slots_v = slots.rearrange("(e p b) w -> e p b w", e=E, p=ROWS)

    def wait_alone(engine, semaphore, value):
        if type(value) is not int:
            engine.compute_val(value)
        engine.wait_ge(consts_in, 32)
        engine.wait_ge(semaphore, value)

    def stream(ctx, cst, wgt):
        def sb(name, shape, dt=f32):
            return ctx.enter_context(nc.sbuf_tensor(name, shape, dt))

        def pb(name, shape):
            return ctx.enter_context(nc.psum_tensor(name, shape, f32))

        def sem(name):
            return ctx.enter_context(nc.semaphore(name))

        h_hi = sb("h_hi", [P, (KT + 1) * D], f32r)
        h_lo = sb("h_lo", [P, (KT + 1) * D], f32r)
        raw = [sb(f"raw{i}", [P, 4 * U]) for i in range(RAW)]
        a_hi = [sb(f"a_hi{i}", [P, 4 * U], f32r) for i in range(SPLIT)]
        a_lo = [sb(f"a_lo{i}", [P, 4 * U], f32r) for i in range(SPLIT)]
        itm = [sb(f"itm{i}", [P, 4 * P]) for i in range(4)]
        fill = sb("fill", [ROWS, BLOCKS * W])
        xin = [sb(f"xin{i}", [TP, TJ, D]) for i in range(2)]
        pay = sb("pay", [TP, TJ, W])
        pay_i = pay[:].bitcast(i32)
        st1 = sb("st1", [TP, TJ, 6])
        st2 = sb("st2", [TP, TJ, 6])
        mv1 = sb("mv1", [TP, TJ, 2])
        mv2 = sb("mv2", [TP, TJ, 2])
        std1 = sb("std1", [TP, TJ])
        std2 = sb("std2", [TP, TJ])
        rstd1 = sb("rstd1", [TP, TJ])
        xn1 = sb("xn1", [TP, TJ, D])
        xn2 = sb("xn2", [TP, TJ, D])
        xn1t = sb("xn1t", [P, U])
        xn2t = sb("xn2t", [P, U])
        rt = sb("rt", [P, U])
        eps = sb("eps", [P, 1])
        logit = sb("logit", [TP, TJ, E])
        lmax = sb("lmax", [TP, TJ])
        ex = sb("ex", [TP, TJ, E])
        esum = sb("esum", [TP, TJ])
        rsum = sb("rsum", [TP, TJ])
        prob = sb("prob", [TP, TJ, E])
        cand = sb("cand", [TP, TJ, E])
        cmax = sb("cmax", [TP, TJ])
        onehot = sb("onehot", [TP, TJ, E])
        rowsum = sb("rowsum", [TP, E])
        carry = sb("carry", [TP, E])
        before = sb("before", [TP, TJ, E])
        over = sb("over", [TP, TJ, E])
        where = sb("where", [TP, TJ, E])
        slot = sb("slot", [TP, TJ])
        slot_i = sb("slot_i", [TP, TJ], i32)
        tok = sb("tok", [TP, TJ])

        acc = [pb(f"acc{i}", [P, U]) for i in range(2)]
        ps_r = pb("ps_r", [TP, TJ, D])
        ps_x1 = pb("ps_x1", [P, U])
        ps_x2 = pb("ps_x2", [P, U])
        ps_l = pb("ps_l", [TP, 64])
        ps_h = [pb(f"ps_h{i}", [P, 4 * D]) for i in range(2)]

        zeroed, filled, fill_set = sem("zeroed"), sem("filled"), sem("fill_set")
        raw_full = [sem(f"raw_full{i}") for i in range(RAW)]
        rest_full = sem("rest_full")
        itm_full = [sem(f"itm_full{i}") for i in range(4)]
        x_full = [sem(f"x_full{i}") for i in range(2)]
        hi_ready, lo_ready, chunk_done, acc_ready = sem("hi_ready"), sem("lo_ready"), sem("chunk_done"), sem("acc_ready")
        h_made, hhi_ready, hlo_ready = sem("h_made"), sem("hhi_ready"), sem("hlo_ready")
        st1_ready, mv1_ready, std1_ready, rstd1_ready = sem("st1_ready"), sem("mv1_ready"), sem("std1_ready"), sem("rstd1_ready")
        xn1_ready, xn1_turned, xn1t_ready = sem("xn1_ready"), sem("xn1_turned"), sem("xn1t_ready")
        relu_ready, relu_turned, x1_ready, x1_stored = sem("relu_ready"), sem("relu_turned"), sem("x1_ready"), sem("x1_stored")
        st2_ready, mv2_ready, std2_ready, rstd2_ready = sem("st2_ready"), sem("mv2_ready"), sem("std2_ready"), sem("rstd2_ready")
        xn2_ready, xn2_turned, xn2t_ready, logits_made = sem("xn2_ready"), sem("xn2_turned"), sem("xn2t_ready"), sem("logits_made")
        route = sem("route")
        shifted_ready, exp_ready, rowsum_ready, counts_made = sem("shifted_ready"), sem("exp_ready"), sem("rowsum_ready"), sem("counts_made")
        slots_ready, scattered = sem("slots_ready"), sem("scattered")
        placed, summed, set_up = sem("placed"), sem("summed"), sem("set_up")
        ROUTE_STEPS = 16

        ident = cst[:, IDENT:IDENT + P]

        def blocks(e, body):
            body(0, 0)
            body(1, 1)
            with e.Fori(1, NB // 2) as i:
                body(i * 2, 0)
                body(i * 2 + 1, 1)

        def width(c):
            return U * (4 if c == 0 else CHUNKS[c])

        block = ctx.enter_context(nc.Block())

        @block.sync
        def _(sp):
            sp.dma_start(cst[:], const).then_inc(consts_in, 16)
            sp.dma_start(wgt[:], weights).then_inc(consts_in, 16)

            def load_item(c):
                if c >= 4:
                    sp.wait_ge(h_made, c - 3)
                n = CHUNKS[c] * P
                sp.dma_start(itm[c % 4][:, 0:n], item_t[:, FIRST[c] * P:FIRST[c] * P + n]).then_inc(itm_full[c % 4], 16)

            def body(u, par):
                first = type(u) is int and u == 0
                for c in range(NC_):
                    if first:
                        load_item(c)
                    if not (first and c < RAW):
                        sp.wait_ge(lo_ready, u * NC_ + (c - RAW + 1))
                    row, at = FIRST[c] // PER_ROW, FIRST[c] % PER_ROW
                    n = CHUNKS[c] * U
                    sp.dma_start(raw[c % RAW][:, 0:n], adj_main[u, row, :, at * U:at * U + n]).then_inc(raw_full[c % RAW], 16)
                    if c == 0:
                        if first:
                            sp.wait_ge(zeroed, 1)
                        sp.dma_start(raw[0][0:REST, 3 * U:4 * U], adj_rest[u, :, :]).then_inc(rest_full, 16)
                    if c == 0:
                        if not (type(u) is int and u < 2):
                            sp.wait_ge(x1_ready, u - 1)
                        sp.dma_start(xin[par][:], x_v[u]).then_inc(x_full[par], 16)
                    if c == 11 and not first:
                        sp.wait_ge(x1_ready, u)
                        sp.dma_start(out_v[u - 1], pay[:, :, 0:D]).then_inc(x1_stored, 16)
                    if first and c >= NC_ - E:
                        if c == NC_ - E:
                            sp.wait_ge(fill_set, 2)
                        sp.dma_start(slots_v[c - (NC_ - E)], fill[:].rearrange("p (b w) -> p b w", w=W)).then_inc(filled, 16)

            blocks(sp, body)
            sp.wait_ge(x1_ready, NB)
            sp.dma_start(out_v[NB - 1], pay[:, :, 0:D]).then_inc(x1_stored, 16)
            sp.wait_ge(x1_stored, 16 * NB)

        @block.scalar
        def _(act):
            def h_high(c):
                act.wait_ge(h_made, c + 1)
                n, at = CHUNKS[c] * D, FIRST[c] * D
                if c == 0:
                    act.wait_ge(set_up, 1)
                    nc.scalar.activation(h_hi[0:REST, KT * D:], ps_h[0][0:REST, 3 * D:4 * D], ACT.Copy)
                nc.scalar.activation(h_hi[:, at:at + n], ps_h[c % 2][:, 0:n], ACT.Copy).then_inc(hhi_ready, 1)

            def split_high(u, c):
                act.wait_ge(raw_full[c % RAW], (u * (NC_ // RAW) + (c // RAW + 1)) * 16)
                if c == 0:
                    act.wait_ge(rest_full, (u + 1) * 16)
                if not (type(u) is int and u == 0 and c < SPLIT):
                    act.wait_ge(chunk_done, u * NC_ + (c - SPLIT + 1))
                nc.scalar.activation(a_hi[c % SPLIT][:, 0:width(c)], raw[c % RAW][:, 0:width(c)], ACT.Copy).then_inc(hi_ready, 1)

            def relu(v, par):
                act.wait_ge(acc_ready, v + 1)
                if not (type(v) is int and v == 0):
                    act.wait_ge(relu_turned, v)
                nc.scalar.activation(rt[:], acc[par][:], ACT.Relu, bias=wgt[:, BUSER:BUSER + 1]).then_inc(relu_ready, 1)

            def std_1(u):
                act.wait_ge(mv1_ready, u + 1)
                nc.scalar.activation(std1[:], mv1[:, :, 1], ACT.Sqrt, bias=eps[0:TP, :]).then_inc(std1_ready, 1)

            def std_2(v):
                act.wait_ge(mv2_ready, v + 1)
                nc.scalar.activation(std2[:], mv2[:, :, 1], ACT.Sqrt, bias=eps[0:TP, :]).then_inc(std2_ready, 1)

            def copy_xn1t(u):
                act.wait_ge(xn1_turned, u + 1)
                if not (type(u) is int and u == 0):
                    act.wait_ge(acc_ready, u)
                nc.scalar.activation(xn1t[:], ps_x1[:], ACT.Copy).then_inc(xn1t_ready, 1)

            def copy_xn2t(v):
                act.wait_ge(xn2_turned, v + 1)
                if not (type(v) is int and v == 0):
                    act.wait_ge(logits_made, v)
                nc.scalar.activation(xn2t[:], ps_x2[:], ACT.Copy).then_inc(xn2t_ready, 1)

            def exp_(v):
                act.wait_ge(shifted_ready, v + 1)
                nc.scalar.activation(ex[:], logit[:], ACT.Exp).then_inc(exp_ready, 1)

            def body(u, par):
                first = type(u) is int and u == 0
                for c in range(NC_):
                    split_high(u, c)
                    if first and c + 2 < NC_:
                        h_high(c + 2)
                    if c == 0 and not first:
                        relu(u - 1, 1 - par)
                    if c == 9:
                        std_1(u)
                        if not first:
                            std_2(u - 1)
                    if c == 13:
                        copy_xn1t(u)
                    if c == 14 and not first:
                        copy_xn2t(u - 1)
                    if c == 19 and not first:
                        exp_(u - 1)

            act.wait_ge(consts_in, 32)
            act.wait_ge(set_up, 1)
            h_high(0)
            h_high(1)
            blocks(act, body)
            relu(NB - 1, 1)
            std_2(NB - 1)
            copy_xn2t(NB - 1)
            exp_(NB - 1)

        @block.vector
        def _(dve):
            nc.vector.memset(raw[0][:, 3 * U:4 * U], 0.0).then_inc(zeroed, 1)
            nc.vector.memset(eps[:], EPS)
            nc.vector.memset(carry[:], 0.0)
            nc.vector.memset(h_hi[:, KT * D:].bitcast(f32), 0.0)
            nc.vector.memset(h_lo[:, KT * D:].bitcast(f32), 0.0).then_inc(set_up, 1)
            nc.vector.memset(fill[:], 0.0).then_inc(fill_set, 1)
            dve.wait_ge(fill_set, 1)
            nc.vector.memset(fill[:].bitcast(i32).rearrange("p (b w) -> p b w", w=W)[:, :, TOKEN], NOWHERE).then_inc(fill_set, 1)
            dve.wait_ge(consts_in, 32)
            nc.vector.tensor_copy(tok[:], cst[0:TP, TOK0:TOK0 + TJ])
            dve.wait_ge(set_up, 1)

            def h_low(c):
                dve.wait_ge(hhi_ready, c + 1)
                n, at = CHUNKS[c] * D, FIRST[c] * D
                if c == 0:
                    nc.vector.tensor_tensor(h_lo[0:REST, KT * D:], ps_h[0][0:REST, 3 * D:4 * D],
                                            h_hi[0:REST, KT * D:].bitcast(f32), ALU.subtract)
                nc.vector.tensor_tensor(h_lo[:, at:at + n], ps_h[c % 2][:, 0:n],
                                        h_hi[:, at:at + n].bitcast(f32), ALU.subtract).then_inc(hlo_ready, 1)

            def split_low(u, c):
                dve.wait_ge(hi_ready, u * NC_ + (c + 1))
                nc.vector.tensor_tensor(a_lo[c % SPLIT][:, 0:width(c)], raw[c % RAW][:, 0:width(c)],
                                        a_hi[c % SPLIT][:, 0:width(c)].bitcast(f32), ALU.subtract).then_inc(lo_ready, 1)

            def stats_1(u, par):
                dve.wait_ge(x_full[par], (u + (2 - par)) * 8)
                for j in range(TJ):
                    last = nc.vector.bn_stats(st1[:, j, :], xin[par][:, j, :])
                last.then_inc(st1_ready, 1)
                wait_alone(dve, st1_ready, u + 1)
                for j in range(TJ):
                    last = nc.vector.bn_aggr(mv1[:, j, :], st1[:, j, :])
                last.then_inc(mv1_ready, 1)

            def norm_1(u, par):
                dve.wait_ge(std1_ready, u + 1)
                nc.vector.reciprocal(rstd1[:], std1[:]).then_inc(rstd1_ready, 1)
                dve.wait_ge(rstd1_ready, u + 1)
                if not (type(u) is int and u == 0):
                    dve.wait_ge(xn1_turned, u)
                for j in range(TJ):
                    last = nc.vector.tensor_scalar(xn1[:, j, :], xin[par][:, j, :], mv1[:, j, 0:1], rstd1[:, j:j + 1],
                                                   ALU.subtract, ALU.mult)
                last.then_inc(xn1_ready, 1)

            def add_x1(v, par):
                dve.wait_ge(relu_turned, v + 1)
                if not (type(v) is int and v == 0):
                    dve.wait_ge(scattered, v * (16 * TJ))
                    dve.wait_ge(x1_stored, v * 16)
                nc.vector.tensor_tensor(pay[:, :, 0:D], ps_r[:], xin[par][:], ALU.add).then_inc(x1_ready, 1)

            def stats_2(v):
                dve.wait_ge(x1_ready, v + 1)
                for j in range(TJ):
                    last = nc.vector.bn_stats(st2[:, j, :], pay[:, j, 0:D])
                last.then_inc(st2_ready, 1)
                wait_alone(dve, st2_ready, v + 1)
                for j in range(TJ):
                    last = nc.vector.bn_aggr(mv2[:, j, :], st2[:, j, :])
                last.then_inc(mv2_ready, 1)

            def norm_2(v):
                dve.wait_ge(std2_ready, v + 1)
                nc.vector.tensor_copy(pay[:, :, MEAN], mv2[:, :, 0])
                nc.vector.reciprocal(pay[:, :, RSTD], std2[:]).then_inc(rstd2_ready, 1)
                dve.wait_ge(rstd2_ready, v + 1)
                if not (type(v) is int and v == 0):
                    dve.wait_ge(xn2_turned, v)
                for j in range(TJ):
                    last = nc.vector.tensor_scalar(xn2[:, j, :], pay[:, j, 0:D], mv2[:, j, 0:1], pay[:, j, RSTD:RSTD + 1],
                                                   ALU.subtract, ALU.mult)
                last.then_inc(xn2_ready, 1)

            def wide(a):
                return a.unsqueeze(2).to_broadcast([TP, TJ, E])

            steps = [0]

            def step(v, instruction):
                steps[0] += 1
                instruction.then_inc(route, 1)
                dve.wait_ge(route, v * ROUTE_STEPS + steps[0])

            def gate_shift(v):
                steps[0] = 0
                dve.wait_ge(logits_made, v + 1)
                gateb = wgt[0:TP, GATEB:GATEB + TJ * E].rearrange("p (j e) -> p j e", e=E)
                step(v, nc.vector.tensor_tensor(logit[:], ps_l[:, 0:TJ * E].rearrange("p (j e) -> p j e", e=E), gateb, ALU.add))
                step(v, nc.vector.reduce_max(lmax[:], logit[:], AX))
                nc.vector.tensor_tensor(logit[:], logit[:], wide(lmax[:]), ALU.subtract).then_inc(shifted_ready, 1)

            def choose(v):
                dve.wait_ge(exp_ready, v + 1)
                step(v, nc.vector.reduce_sum(esum[:], ex[:], AX))
                step(v, nc.vector.reciprocal(rsum[:], esum[:]))
                step(v, nc.vector.tensor_tensor(prob[:], ex[:], wide(rsum[:]), ALU.mult))
                step(v, nc.vector.reduce_max(pay[:, :, PROB], prob[:], AX))
                step(v, nc.vector.tensor_tensor(cand[:], prob[:], wide(pay[:, :, PROB]), ALU.is_equal))
                step(v, nc.vector.tensor_tensor(cand[:], cand[:], cst[0:TP, REV:REV + TJ * E].rearrange("p (j e) -> p j e", e=E), ALU.mult))
                step(v, nc.vector.reduce_max(cmax[:], cand[:], AX))
                step(v, nc.vector.tensor_tensor(onehot[:], cand[:], wide(cmax[:]), ALU.is_equal))
                nc.vector.reduce_sum(rowsum[:], onehot[:].rearrange("p j e -> p e j"), AX).then_inc(rowsum_ready, 1)

            def place(v):
                dve.wait_ge(counts_made, v + 1)
                step(v, nc.vector.tensor_tensor(before[:, 0, :], ps_l[:, 32:32 + E], carry[:], ALU.add))
                for j in range(1, TJ):
                    step(v, nc.vector.tensor_tensor(before[:, j, :], before[:, j - 1, :], onehot[:, j - 1, :], ALU.add))
                nc.vector.tensor_tensor(carry[:], carry[:], ps_l[:, 40:40 + E], ALU.add)
                nc.vector.tensor_scalar(over[:], before[:], float(C), float(NOWHERE), ALU.is_ge, ALU.mult)
                step(v, nc.vector.tensor_tensor(where[:], before[:], cst[0:TP, EOFF:EOFF + TJ * E].rearrange("p (j e) -> p j e", e=E), ALU.add))
                step(v, nc.vector.tensor_tensor(where[:], where[:], over[:], ALU.add))
                nc.vector.tensor_copy(pay_i[:, :, TOKEN], tok[:])
                nc.vector.tensor_scalar(tok[:], tok[:], float(U), None, ALU.add)
                nc.vector.tensor_tensor(where[:], where[:], onehot[:], ALU.mult).then_inc(placed, 1)
                dve.wait_ge(placed, v + 1)
                nc.vector.reduce_sum(slot[:], where[:], AX).then_inc(summed, 1)
                dve.wait_ge(summed, v + 1)
                nc.vector.tensor_copy(slot_i[:], slot[:]).then_inc(slots_ready, 1)
                assert steps[0] == ROUTE_STEPS, steps[0]

            def body(u, par):
                first = type(u) is int and u == 0
                for c in range(NC_):
                    split_low(u, c)
                    if first and c + 2 < NC_:
                        h_low(c + 2)
                    if c == 3:
                        stats_1(u, par)
                    if c == 5 and not first:
                        add_x1(u - 1, 1 - par)
                    if c == 6 and not first:
                        stats_2(u - 1)
                    if c == 10:
                        norm_1(u, par)
                    if c == 11 and not first:
                        norm_2(u - 1)
                    if c == 17 and not first:
                        gate_shift(u - 1)
                    if c == 20 and not first:
                        choose(u - 1)
                    if c == 22 and not first:
                        place(u - 1)

            h_low(0)
            h_low(1)
            blocks(dve, body)
            add_x1(NB - 1, 1)
            stats_2(NB - 1)
            norm_2(NB - 1)
            gate_shift(NB - 1)
            choose(NB - 1)
            place(NB - 1)

        @block.tensor
        def _(pe):
            def make_h(c):
                pe.wait_ge(itm_full[c % 4], (c // 4 + 1) * 16)
                if c >= 2:
                    pe.wait_ge(hlo_ready, c - 1)
                for k in range(CHUNKS[c]):
                    o = ps_h[c % 2][:, k * D:(k + 1) * D]
                    nc.tensor.matmul(o, itm[c % 4][:, k * P:(k + 1) * P], wgt[:, WIT:WIT + D], start=True, stop=False)
                    last = nc.tensor.matmul(o, cst[:, ONES:ONES + P], wgt[:, BITEM:BITEM + D], start=False, stop=True)
                if c == 0:
                    o = ps_h[0][0:REST, 3 * D:4 * D]
                    nc.tensor.matmul(o, wgt[:, ITREST:ITREST + REST], wgt[:, WIT:WIT + D], start=True, stop=False)
                    last = nc.tensor.matmul(o, cst[:, ONES:ONES + REST], wgt[:, BITEM:BITEM + D], start=False, stop=True)
                last.then_inc(h_made, 1)

            def products(u, par, c):
                first = type(u) is int and u == 0
                if first:
                    pe.wait_ge(hlo_ready, c + 1)
                pe.wait_ge(lo_ready, u * NC_ + (c + 1))
                if c == 0 and not (type(u) is int and u < 2):
                    pe.wait_ge(relu_ready, u - 1)
                tiles = [(k, FIRST[c] + k) for k in range(CHUNKS[c])] + [(3, KT)] * (c == 0)
                for k, t in tiles:
                    hi, lo = a_hi[c % SPLIT][:, k * U:(k + 1) * U], a_lo[c % SPLIT][:, k * U:(k + 1) * U]
                    wh, wl = h_hi[:, t * D:(t + 1) * D], h_lo[:, t * D:(t + 1) * D]
                    nc.tensor.matmul(acc[par][:], wh, hi, start=(c == 0 and k == 0), stop=False)
                    nc.tensor.matmul(acc[par][:], wh, lo, start=False, stop=False)
                    last = nc.tensor.matmul(acc[par][:], wl, hi, start=False, stop=False)
                last.then_inc(chunk_done, 1)

            def user_part(u, par):
                pe.wait_ge(xn1t_ready, u + 1)
                nc.tensor.matmul(acc[par][:], wgt[:, WUT:WUT + D], xn1t[:], start=False, stop=True).then_inc(acc_ready, 1)

            def turn_xn1(u):
                pe.wait_ge(xn1_ready, u + 1)
                for j in range(TJ):
                    last = nc.tensor.transpose(ps_x1[:, j * TP:(j + 1) * TP], xn1[:, j, :], ident[0:TP, 0:TP])
                last.then_inc(xn1_turned, 1)

            def turn_relu(v):
                pe.wait_ge(relu_ready, v + 1)
                for j in range(TJ):
                    last = nc.tensor.transpose(ps_r[:, j, :], rt[:, j * TP:(j + 1) * TP], ident)
                last.then_inc(relu_turned, 1)

            def turn_xn2(v):
                pe.wait_ge(xn2_ready, v + 1)
                for j in range(TJ):
                    last = nc.tensor.transpose(ps_x2[:, j * TP:(j + 1) * TP], xn2[:, j, :], ident[0:TP, 0:TP])
                last.then_inc(xn2_turned, 1)

            def logits(v):
                pe.wait_ge(xn2t_ready, v + 1)
                for j in range(TJ):
                    last = nc.tensor.matmul(ps_l[:, j * E:(j + 1) * E], xn2t[:, j * TP:(j + 1) * TP], wgt[:, GATEW:GATEW + E],
                                            start=True, stop=True)
                last.then_inc(logits_made, 1)

            def count(v):
                pe.wait_ge(rowsum_ready, v + 1)
                nc.tensor.matmul(ps_l[:, 32:32 + E], cst[0:TP, TRI:TRI + TP], rowsum[:], start=True, stop=True)
                nc.tensor.matmul(ps_l[:, 40:40 + E], cst[0:TP, ONES:ONES + TP], rowsum[:], start=True, stop=True).then_inc(counts_made, 1)

            def body(u, par):
                first = type(u) is int and u == 0
                for c in range(NC_):
                    if first and c + 2 < NC_:
                        make_h(c + 2)
                    products(u, par, c)
                    if c == 2 and not first:
                        turn_relu(u - 1)
                    if c == 11:
                        turn_xn1(u)
                    if c == 12 and not first:
                        turn_xn2(u - 1)
                    if c == 15 and not first:
                        logits(u - 1)
                    if c == 21 and not first:
                        count(u - 1)
                user_part(u, par)

            pe.wait_ge(consts_in, 32)
            make_h(0)
            make_h(1)
            blocks(pe, body)
            turn_relu(NB - 1)
            turn_xn2(NB - 1)
            logits(NB - 1)
            count(NB - 1)

        @block.gpsimd
        def _(pool):
            def scatter(v):
                wait_alone(pool, slots_ready, v + 1)
                for j in range(TJ):
                    nc.gpsimd.indirect_dma_start(slots, bass.IndirectOffsetOnAxis(ap=slot_i[:, j:j + 1], axis=0),
                                                 pay[:, j, :], None, bounds_check=E * CP - 1,
                                                 oob_is_err=False).then_inc(scattered, 16)

            pool.wait_ge(filled, 16 * E)
            with pool.Fori(0, NB) as v:
                scatter(v)
            pool.wait_ge(scattered, 16 * TJ * NB)

    def experts(ctx, cst, wgt):
        def sb(name, shape, dt=f32):
            return ctx.enter_context(nc.sbuf_tensor(name, shape, dt))

        def pb(name, shape):
            return ctx.enter_context(nc.psum_tensor(name, shape, f32))

        def sem(name):
            return ctx.enter_context(nc.semaphore(name))

        GC = max(GROUPS) * ROWS
        w1r = [sb(f"w1r{i}", [P, F]) for i in range(2)]
        w2r = [sb(f"w2r{i}", [P, FC, D]) for i in range(2)]
        w1h = [sb(f"w1h{i}", [P, F], f32r) for i in range(2)]
        w1l = [sb(f"w1l{i}", [P, F], f32r) for i in range(2)]
        w2h = [sb(f"w2h{i}", [P, FC, D], f32r) for i in range(2)]
        w2l = [sb(f"w2l{i}", [P, FC, D], f32r) for i in range(2)]
        natx = [sb(f"natx{i}", [ROWS, BLOCKS, W]) for i in range(2)]
        natr = [sb(f"natr{i}", [ROWS, BLOCKS, W]) for i in range(2)]
        xs = [sb(f"xs{i}", [ROWS, BLOCKS, D]) for i in range(2)]
        xh = [sb(f"xh{i}", [P, CP], f32r) for i in range(2)]
        xl = [sb(f"xl{i}", [P, CP], f32r) for i in range(2)]
        hr = [sb(f"hr{i}", [P, FC, GC]) for i in range(2)]
        hh = [sb(f"hh{i}", [P, FC, GC], f32r) for i in range(2)]
        hl = [sb(f"hl{i}", [P, FC, GC], f32r) for i in range(2)]
        yt = [sb(f"yt{i}", [P, GC]) for i in range(2)]
        y = sb("y", [ROWS, 4, D])
        posv = sb("posv", [ROWS, 4, D])
        negv = sb("negv", [ROWS, 4, D])
        diff = sb("diff", [ROWS, 4, D])
        mask = sb("mask", [ROWS, 4, D], i32)
        res = [sb(f"res{i}", [ROWS, 4, D]) for i in range(2)]

        ps_1 = [pb(f"ps_1{i}", [P, GC]) for i in range(FC)]
        ps_x = pb("ps_x", [P, GC])
        ps_y = pb("ps_y", [P, GC])
        ps_o = [pb(f"ps_o{i}", [ROWS, 4, D]) for i in range(2)]

        w_full = [sem(f"w_full{i}") for i in range(2)]
        natx_full = [sem(f"natx_full{i}") for i in range(2)]
        natr_full = [sem(f"natr_full{i}") for i in range(2)]
        whi_ready, wlo_ready, xs_ready, x_turned = sem("whi_ready"), sem("wlo_ready"), sem("xs_ready"), sem("x_turned")
        xh_ready, xl_ready, up_made, relu_done = sem("xh_ready"), sem("xl_ready"), sem("up_made"), sem("relu_done")
        hh_ready, hl_ready, down_made, yt_ready = sem("hh_ready"), sem("hl_ready"), sem("down_made"), sem("yt_ready")
        y_turned, y_ready, signs, zeros_ready = sem("y_turned"), sem("y_ready"), sem("signs"), sem("zeros_ready")
        guard, guarded, res_ready = sem("guard"), sem("guarded"), sem("res_ready")
        written = [sem(f"written{i}") for i in range(2)]
        ident = cst[:, IDENT:IDENT + P]

        def each(e, body):
            body(0, 0)
            with e.Fori(0, (E - 2) // 2) as i:
                body(i * 2 + 1, 1)
                body(i * 2 + 2, 0)
            body(E - 1, 1)

        def at(n, least):
            return not (type(n) is int and n < least)

        def of(e, par):
            return (e // 2 + 1) * 16 if type(e) is int else (e + (2 - par)) * 8

        def cols(g):
            return GFIRST[g] * ROWS, GROUPS[g] * ROWS

        def written_by(e, g, b):
            whole = 16 * sum(GROUPS[k] for k in range(b, G, 2))
            return e * whole + 16 * sum(GROUPS[k] for k in range(b, g, 2))

        block = ctx.enter_context(nc.Block())

        @block.sync
        def _(sp):
            def load_w(e, q):
                if at(e, 2):
                    sp.wait_ge(wlo_ready, e - 1)
                sp.dma_start(w1r[q][:], w1[e]).then_inc(w_full[q], 16)
                sp.dma_start(w2r[q][:], w2[e].rearrange("(f p) d -> p f d", p=P)).then_inc(w_full[q], 16)

            def load_x(e, q):
                if at(e, 2):
                    sp.wait_ge(xs_ready, e * G - G)
                sp.dma_start(natx[q][:], slots_v[e]).then_inc(natx_full[q], 16)

            def load_r(e, q):
                if at(e, 2):
                    sp.wait_ge(written[0], written_by(e - 1, 0, 0))
                    sp.wait_ge(written[1], written_by(e - 1, 0, 1))
                sp.dma_start(natr[q][:], slots_v[e]).then_inc(natr_full[q], 16)

            def body(e, q):
                if not (type(e) is int and e == E - 1):
                    load_w(e + 1, 1 - q)
                    load_x(e + 1, 1 - q)
                    load_r(e + 1, 1 - q)

            load_x(0, 0)
            load_w(0, 0)
            load_r(0, 0)
            each(sp, body)

        def bcast(a, nb):
            return a.to_broadcast([ROWS, nb, D])

        @block.scalar
        def _(act):
            def w_high(e, q):
                act.wait_ge(w_full[q], of(e, q) * 2)
                if at(e, 2):
                    act.wait_ge(down_made, e * G - G)
                nc.scalar.activation(w1h[q][:], w1r[q][:], ACT.Copy)
                nc.scalar.activation(w2h[q][:], w2r[q][:], ACT.Copy).then_inc(whi_ready, 1)

            def x_high(e, q, g):
                c0, n = cols(g)
                act.wait_ge(x_turned, e * G + (g + 1))
                if at(e, 2):
                    act.wait_ge(up_made, e * (G * FC) - G * FC)
                nc.scalar.activation(xh[q][:, c0:c0 + n], ps_x[:, 0:n], ACT.Copy).then_inc(xh_ready, 1)

            def relu(e, q, g):
                _, n = cols(g)
                if not (type(e) is int and e == 0 and g < 2):
                    act.wait_ge(hl_ready, e * G + (g - 1))
                for f in range(FC):
                    wait_alone(act, up_made, e * (G * FC) + (g * FC + f + 1))
                    nc.scalar.activation(hr[g % 2][:, f, 0:n], ps_1[f][:, 0:n], ACT.Relu,
                                         bias=b1_of(e, f)).then_inc(relu_done, 1)

            def y_out(e, g):
                _, n = cols(g)
                wait_alone(act, down_made, e * G + (g + 1))
                if not (type(e) is int and e == 0 and g < 2):
                    wait_alone(act, y_turned, e * G + (g - 1))
                nc.scalar.activation(yt[g % 2][:, 0:n], ps_y[:, 0:n], ACT.Identity,
                                     bias=b2_of(e)).then_inc(yt_ready, 1)

            def b1_of(e, f):
                o = e * FC + (B1 + f)
                return wgt[:, o:o + 1] if type(e) is int else wgt[:, bass.ds(o, 1)]

            def b2_of(e):
                o = e + B2
                return wgt[:, o:o + 1] if type(e) is int else wgt[:, bass.ds(o, 1)]

            def body(e, q):
                for g in range(G):
                    relu(e, q, g)
                    if not (type(e) is int and e == E - 1):
                        x_high(e + 1, 1 - q, g)
                        if g == 2:
                            w_high(e + 1, 1 - q)
                    if g > 0:
                        y_out(e, g - 1)
                    elif not (type(e) is int and e == 0):
                        y_out(e - 1, G - 1)

            w_high(0, 0)
            for g in range(G):
                x_high(0, 0, g)
            each(act, body)
            y_out(E - 1, G - 1)

        @block.vector
        def _(dve):
            def w_low(e, q):
                dve.wait_ge(whi_ready, e + 1)
                nc.vector.tensor_tensor(w1l[q][:], w1r[q][:], w1h[q][:].bitcast(f32), ALU.subtract)
                nc.vector.tensor_tensor(w2l[q][:], w2r[q][:], w2h[q][:].bitcast(f32), ALU.subtract).then_inc(wlo_ready, 1)

            def x_low(e, q, g):
                c0, n = cols(g)
                dve.wait_ge(xh_ready, e * G + (g + 1))
                nc.vector.tensor_tensor(xl[q][:, c0:c0 + n], ps_x[:, 0:n], xh[q][:, c0:c0 + n].bitcast(f32),
                                        ALU.subtract).then_inc(xl_ready, 1)

            def split_h(e, g):
                _, n = cols(g)
                b = g % 2
                dve.wait_ge(relu_done, e * (G * FC) + (g + 1) * FC)
                if not (type(e) is int and e == 0 and g < 2):
                    dve.wait_ge(down_made, e * G + (g - 1))
                nc.vector.tensor_copy(hh[b][:, :, 0:n], hr[b][:, :, 0:n]).then_inc(hh_ready, 1)
                dve.wait_ge(hh_ready, e * G + (g + 1))
                nc.vector.tensor_tensor(hl[b][:, :, 0:n], hr[b][:, :, 0:n], hh[b][:, :, 0:n].bitcast(f32),
                                        ALU.subtract).then_inc(hl_ready, 1)

            def result(e, q, g):
                nb, b0, b = GROUPS[g], GFIRST[g], g % 2
                k = e * G + (g + 1)
                if g == 0:
                    dve.wait_ge(natr_full[q], of(e, q))
                dve.wait_ge(y_turned, k)
                nc.vector.tensor_tensor(y[:, 0:nb], ps_o[b][:, 0:nb], bcast(natr[q][:, b0:b0 + nb, PROB:PROB + 1], nb),
                                        ALU.mult).then_inc(y_ready, 1)
                dve.wait_ge(y_ready, k)
                nc.vector.tensor_scalar(posv[:, 0:nb], y[:, 0:nb], 0.0, 1e4, ALU.is_gt, ALU.mult)
                nc.vector.tensor_scalar(negv[:, 0:nb], y[:, 0:nb], 0.0, 1e4, ALU.is_lt, ALU.mult)
                nc.vector.tensor_tensor(diff[:, 0:nb], y[:, 0:nb], y[:, 0:nb], ALU.subtract).then_inc(signs, 1)
                dve.wait_ge(signs, k)
                nc.vector.tensor_tensor(posv[:, 0:nb], posv[:, 0:nb], negv[:, 0:nb], ALU.subtract)
                nc.vector.tensor_scalar(mask[:, 0:nb], diff[:, 0:nb], 0.0, None, ALU.is_equal).then_inc(guard, 1)
                wait_alone(dve, guard, k)
                nc.vector.copy_predicated(posv[:, 0:nb], mask[:, 0:nb], y[:, 0:nb]).then_inc(guarded, 1)
                dve.wait_ge(guarded, k)
                if not (type(e) is int and e == 0 and g < 2):
                    dve.wait_ge(written[b], written_by(e, g, b))
                nc.vector.tensor_tensor(res[b][:, 0:nb], posv[:, 0:nb], natr[q][:, b0:b0 + nb, 0:D], ALU.add).then_inc(res_ready, 1)

            def body(e, q):
                for g in range(G):
                    split_h(e, g)
                    if not (type(e) is int and e == E - 1):
                        x_low(e + 1, 1 - q, g)
                        if g == 2:
                            w_low(e + 1, 1 - q)
                    if g > 1:
                        result(e, q, g - 2)
                    elif not (type(e) is int and e == 0):
                        result(e - 1, 1 - q, G - 2 + g)

            w_low(0, 0)
            for g in range(G):
                x_low(0, 0, g)
            each(dve, body)
            result(E - 1, 1, G - 2)
            result(E - 1, 1, G - 1)

        @block.tensor
        def _(pe):
            def turn_x(e, q, g):
                pe.wait_ge(xs_ready, e * G + (g + 1))
                if not (type(e) is int and e == 0 and g == 0):
                    pe.wait_ge(xl_ready, e * G + g)
                for k in range(GROUPS[g]):
                    last = nc.tensor.transpose(ps_x[:, k * ROWS:(k + 1) * ROWS], xs[q][:, GFIRST[g] + k, :],
                                               ident[0:ROWS, 0:ROWS])
                last.then_inc(x_turned, 1)

            def up(e, q, g):
                c0, n = cols(g)
                if g == 0:
                    pe.wait_ge(wlo_ready, e + 1)
                pe.wait_ge(xl_ready, e * G + (g + 1))
                for f in range(FC):
                    if not (type(e) is int and e == 0 and g == 0):
                        pe.wait_ge(relu_done, e * (G * FC) + ((g - 1) * FC + f + 1))
                    wh, wl = w1h[q][:, f * P:(f + 1) * P], w1l[q][:, f * P:(f + 1) * P]
                    o = ps_1[f][:, 0:n]
                    nc.tensor.matmul(o, wh, xh[q][:, c0:c0 + n], start=True, stop=False)
                    nc.tensor.matmul(o, wh, xl[q][:, c0:c0 + n], start=False, stop=False)
                    nc.tensor.matmul(o, wl, xh[q][:, c0:c0 + n], start=False, stop=True).then_inc(up_made, 1)

            def down(e, q, g):
                _, n = cols(g)
                b = g % 2
                pe.wait_ge(hl_ready, e * G + (g + 1))
                if not (type(e) is int and e == 0 and g == 0):
                    pe.wait_ge(yt_ready, e * G + g)
                for f in range(FC):
                    o = ps_y[:, 0:n]
                    hi, lo = hh[b][:, f, 0:n], hl[b][:, f, 0:n]
                    nc.tensor.matmul(o, w2h[q][:, f, :], hi, start=(f == 0), stop=False)
                    nc.tensor.matmul(o, w2h[q][:, f, :], lo, start=False, stop=False)
                    last = nc.tensor.matmul(o, w2l[q][:, f, :], hi, start=False, stop=(f == FC - 1))
                last.then_inc(down_made, 1)

            def turn_y(e, g):
                b = g % 2
                pe.wait_ge(yt_ready, e * G + (g + 1))
                if not (type(e) is int and e == 0 and g < 2):
                    pe.wait_ge(y_ready, e * G + (g - 1))
                for k in range(GROUPS[g]):
                    last = nc.tensor.transpose(ps_o[b][:, k, :], yt[b][:, k * ROWS:(k + 1) * ROWS], ident)
                last.then_inc(y_turned, 1)

            def body(e, q):
                for g in range(G):
                    up(e, q, g)
                    if not (type(e) is int and e == E - 1):
                        turn_x(e + 1, 1 - q, g)
                    if g > 0:
                        down(e, q, g - 1)
                    elif not (type(e) is int and e == 0):
                        down(e - 1, 1 - q, G - 1)
                    if g > 1:
                        turn_y(e, g - 2)
                    elif not (type(e) is int and e == 0):
                        turn_y(e - 1, G - 2 + g)

            for g in range(G):
                turn_x(0, 0, g)
            each(pe, body)
            down(E - 1, 1, G - 1)
            turn_y(E - 1, G - 2)
            turn_y(E - 1, G - 1)

        @block.gpsimd
        def _(pool):
            def normalise(e, q, g):
                if g == 0:
                    wait_alone(pool, natx_full[q], of(e, q))
                    if at(e, 2):
                        wait_alone(pool, x_turned, e * G - G)
                for k in range(GFIRST[g], GFIRST[g] + GROUPS[g]):
                    last = nc.gpsimd.tensor_scalar(xs[q][:, k, :], natx[q][:, k, 0:D], natx[q][:, k, MEAN:MEAN + 1],
                                                   natx[q][:, k, RSTD:RSTD + 1], ALU.subtract, ALU.mult)
                last.then_inc(xs_ready, 1)

            def write(e, q, g):
                wait_alone(pool, res_ready, e * G + (g + 1))
                for k in range(GROUPS[g]):
                    token = natr[q][:].bitcast(i32)[:, GFIRST[g] + k, TOKEN:TOKEN + 1]
                    nc.gpsimd.indirect_dma_start(out, bass.IndirectOffsetOnAxis(ap=token, axis=0), res[g % 2][:, k, :], None,
                                                 bounds_check=T - 1, oob_is_err=False).then_inc(written[g % 2], 16)

            def body(e, q):
                for g in range(G):
                    if not (type(e) is int and e == E - 1):
                        normalise(e + 1, 1 - q, g)
                    if g > 1:
                        write(e, q, g - 2)
                    elif not (type(e) is int and e == 0):
                        write(e - 1, 1 - q, G - 2 + g)

            for g in range(G):
                normalise(0, 0, g)
            each(pool, body)
            write(E - 1, 1, G - 2)
            write(E - 1, 1, G - 1)
            for b in range(2):
                pool.wait_ge(written[b], written_by(E, 0, b))

    with ExitStack() as ctx:
        consts_in = ctx.enter_context(nc.semaphore("consts_in"))
        cst = ctx.enter_context(nc.sbuf_tensor("cst", [P, CONST_W], f32))
        wgt = ctx.enter_context(nc.sbuf_tensor("wgt", [P, WEIGHT_W], f32))
        with ExitStack() as inner:
            stream(inner, cst, wgt)
        with ExitStack() as inner:
            experts(inner, cst, wgt)


def kernel(x, adj, L0_gnn_item_feat, L0_gnn_W_item, L0_gnn_b_item, L0_gnn_W_user, L0_gnn_b_user,
           L0_ffn_gate_w, L0_ffn_gate_b, L0_ffn_w1, L0_ffn_b1, L0_ffn_w2, L0_ffn_b2):
    import numpy as np
    import concourse.bacc as bacc
    from concourse.bass_utils import run_bass_kernel_spmd

    f = np.float32
    a = np.asarray(adj).reshape(NB, TP, TJ, N)
    main = np.empty((NB, KT // PER_ROW, P, PER_ROW, TJ, TP), f)
    for u in range(NB):
        t = np.ascontiguousarray(a[u].transpose(2, 1, 0))
        main[u] = t[:KT * P].reshape(KT // PER_ROW, PER_ROW, P, TJ, TP).transpose(0, 2, 1, 3, 4)
    rest = np.ascontiguousarray(a[:, :, :, KT * P:].transpose(0, 3, 2, 1)).reshape(NB, REST, U)
    item_t = np.ascontiguousarray(np.asarray(L0_gnn_item_feat).T)

    const = np.zeros((P, CONST_W), f)
    const[:, IDENT:IDENT + P] = np.eye(P)
    const[:, TRI:TRI + P] = np.triu(np.ones((P, P)), 1)
    const[:, ONES:ONES + P] = 1.0
    const[:, REV:REV + TJ * E] = np.tile(np.arange(E, 0, -1), TJ)
    const[:, EOFF:EOFF + TJ * E] = np.tile(np.arange(E) * CP, TJ)
    const[:, TOK0:TOK0 + TJ] = np.arange(P)[:, None] * TJ + np.arange(TJ)

    weights = np.zeros((P, WEIGHT_W), f)
    weights[:, WIT:WIT + D] = np.asarray(L0_gnn_W_item).T
    weights[:, WUT:WUT + D] = np.asarray(L0_gnn_W_user).T
    weights[0, BITEM:BITEM + D] = L0_gnn_b_item
    weights[:, ITREST:ITREST + REST] = item_t[:, KT * P:]
    weights[:, GATEW:GATEW + E] = L0_ffn_gate_w
    weights[:, GATEB:GATEB + TJ * E] = np.tile(np.asarray(L0_ffn_gate_b), TJ)
    weights[:, BUSER] = L0_gnn_b_user
    weights[:, B1:B1 + E * FC] = np.asarray(L0_ffn_b1).reshape(E * FC, P).T
    weights[:, B2:B2 + E] = np.asarray(L0_ffn_b2).T

    arrays = {
        "adj_main": main.reshape(NB, KT // PER_ROW, P, PER_ROW * U), "adj_rest": rest, "x_in": np.ascontiguousarray(x),
        "item_t": item_t, "const": const, "weights": weights,
        "w1_in": np.ascontiguousarray(L0_ffn_w1), "w2_in": np.ascontiguousarray(L0_ffn_w2),
    }
    nc = bacc.Bacc("TRN2", target_bir_lowering=False, num_devices=1)
    args = [nc.dram_tensor(k, v.shape, mybir.dt.from_np(v.dtype), kind="ExternalInput").ap() for k, v in arrays.items()]
    out = nc.dram_tensor("out", (T, D), mybir.dt.float32, kind="ExternalOutput").ap()
    build(nc, *args, out)
    return run_bass_kernel_spmd(nc, [arrays], core_ids=[0]).results[0]["out"]
```

```python
import concourse.bass as bass
from concourse import mybir
from contextlib import ExitStack

P = 128
T = 10000
N = 10000
D = 128
E = 8
F = 512
FC = F // P
C = 1563
EPS = 1e-5

U = 500
NB = T // U
TP = 125
TJ = U // TP
KT = N // P
REST = N - KT * P
CT = 2
FULL = KT // CT
CHUNKS = FULL + 1
PER_ROW = 26
RAW = 10
SPLIT = 5
AHEAD = 2

ROWS = 112
BLOCKS = 14
CP = ROWS * BLOCKS
GROUPS = [4, 4, 3, 3]
GFIRST = [0, 4, 8, 11]
G = len(GROUPS)
W = 132
MEAN, RSTD, PROB, TOKEN = 128, 129, 130, 131
NOWHERE = 1 << 20

IDENT, TRI, ONES, REV, EOFF, TOK0, CONST_W = 0, 128, 256, 384, 416, 448, 452
WIT, WUT, BITEM, ITREST, GATEW, GATEB, BUSER, B1, B2, WEIGHT_W = 0, 128, 256, 384, 400, 408, 440, 441, 473, 481


def build(nc, adj_main, adj_rest, x, item_t, const, weights, w1, w2, out):
    f32, f32r, i32 = mybir.dt.float32, mybir.dt.float32r, mybir.dt.int32
    ALU, ACT, AX = mybir.AluOpType, mybir.ActivationFunctionType, mybir.AxisListType.X

    slots = nc.dram_tensor("slots", (E * CP, W), f32, kind="Internal").ap()
    x_v = x.rearrange("(u p j) d -> u p j d", p=TP, j=TJ)
    out_v = out.rearrange("(u p j) d -> u p j d", p=TP, j=TJ)
    slots_v = slots.rearrange("(e p b) w -> e p b w", e=E, p=ROWS)
    slots_b = slots.rearrange("(e p b) w -> e b p w", e=E, p=ROWS)
    y_all = nc.dram_tensor("y_all", (E, P, CP), f32, kind="Internal").ap()

    def wait_alone(engine, semaphore, value):
        if type(value) is not int:
            engine.compute_val(value)
        engine.wait_ge(consts_in, 32)
        engine.wait_ge(semaphore, value)

    def stream(ctx, cst, wgt):
        def sb(name, shape, dt=f32):
            return ctx.enter_context(nc.sbuf_tensor(name, shape, dt))

        def pb(name, shape):
            return ctx.enter_context(nc.psum_tensor(name, shape, f32))

        def sem(name):
            return ctx.enter_context(nc.semaphore(name))

        h_hi = sb("h_hi", [P, (KT + 1) * D], f32r)
        h_lo = sb("h_lo", [P, (KT + 1) * D], f32r)
        raw = [sb(f"raw{i}", [P, CT * U]) for i in range(RAW)]
        raw_rest = sb("raw_rest", [P, U])
        a_hi = [sb(f"a_hi{i}", [P, CT * U], f32r) for i in range(SPLIT)]
        a_lo = [sb(f"a_lo{i}", [P, CT * U], f32r) for i in range(SPLIT)]
        itm = [sb(f"itm{i}", [P, CT * P]) for i in range(4)]
        fill = sb("fill", [ROWS, BLOCKS * W])
        xin = [sb(f"xin{i}", [TP, TJ, D]) for i in range(2)]
        pay = sb("pay", [TP, TJ, W])
        pay_i = pay[:].bitcast(i32)
        st1 = sb("st1", [TP, TJ, 6])
        st2 = sb("st2", [TP, TJ, 6])
        mv1 = sb("mv1", [TP, TJ, 2])
        mv2 = sb("mv2", [TP, TJ, 2])
        std1 = sb("std1", [TP, TJ])
        std2 = sb("std2", [TP, TJ])
        rstd1 = sb("rstd1", [TP, TJ])
        xn1 = sb("xn1", [TP, TJ, D])
        xn2 = sb("xn2", [TP, TJ, D])
        xn1t = sb("xn1t", [P, U])
        xn2t = sb("xn2t", [P, U])
        rt = sb("rt", [P, U])
        eps = sb("eps", [P, 1])
        logit = sb("logit", [TP, TJ, E])
        lmax = sb("lmax", [TP, TJ])
        ex = sb("ex", [TP, TJ, E])
        esum = sb("esum", [TP, TJ])
        rsum = sb("rsum", [TP, TJ])
        prob = sb("prob", [TP, TJ, E])
        cand = sb("cand", [TP, TJ, E])
        cmax = sb("cmax", [TP, TJ])
        onehot = sb("onehot", [TP, TJ, E])
        rowsum = sb("rowsum", [TP, E])
        carry = sb("carry", [TP, E])
        before = sb("before", [TP, TJ, E])
        over = sb("over", [TP, TJ, E])
        where = sb("where", [TP, TJ, E])
        slot = sb("slot", [TP, TJ])
        slot_i = sb("slot_i", [TP, TJ], i32)
        tok = sb("tok", [TP, TJ])

        acc = [pb(f"acc{i}", [P, U]) for i in range(2)]
        ps_r = pb("ps_r", [TP, TJ, D])
        ps_x1 = pb("ps_x1", [P, U])
        ps_x2 = pb("ps_x2", [P, U])
        ps_l = pb("ps_l", [TP, 64])
        ps_h = [pb(f"ps_h{i}", [P, CT * D]) for i in range(2)]

        zeroed, filled, fill_set = sem("zeroed"), sem("filled"), sem("fill_set")
        raw_full = [sem(f"raw_full{i}") for i in range(RAW)]
        rest_full = sem("rest_full")
        itm_full = [sem(f"itm_full{i}") for i in range(4)]
        x_full = [sem(f"x_full{i}") for i in range(2)]
        hi_ready, lo_ready, chunk_done, acc_ready = sem("hi_ready"), sem("lo_ready"), sem("chunk_done"), sem("acc_ready")
        h_made, hhi_ready, hlo_ready = sem("h_made"), sem("hhi_ready"), sem("hlo_ready")
        st1_ready, mv1_ready, std1_ready, rstd1_ready = sem("st1_ready"), sem("mv1_ready"), sem("std1_ready"), sem("rstd1_ready")
        xn1_ready, xn1_turned, xn1t_ready = sem("xn1_ready"), sem("xn1_turned"), sem("xn1t_ready")
        relu_ready, relu_turned, x1_ready, x1_stored = sem("relu_ready"), sem("relu_turned"), sem("x1_ready"), sem("x1_stored")
        st2_ready, mv2_ready, std2_ready, rstd2_ready = sem("st2_ready"), sem("mv2_ready"), sem("std2_ready"), sem("rstd2_ready")
        xn2_ready, xn2_turned, xn2t_ready, logits_made = sem("xn2_ready"), sem("xn2_turned"), sem("xn2t_ready"), sem("logits_made")
        route = sem("route")
        shifted_ready, exp_ready, rowsum_ready, counts_made = sem("shifted_ready"), sem("exp_ready"), sem("rowsum_ready"), sem("counts_made")
        slots_ready, scattered = sem("slots_ready"), sem("scattered")
        placed, summed, set_up = sem("placed"), sem("summed"), sem("set_up")
        ROUTE_STEPS = 16

        ident = cst[:, IDENT:IDENT + P]

        def blocks(e, body):
            body(0, 0)
            body(1, 1)
            with e.Fori(1, NB // 2) as i:
                body(i * 2, 0)
                body(i * 2 + 1, 1)

        def tiles(c):
            return CT if c < FULL else 1

        def source(c):
            return raw[c % RAW][:] if c < FULL else raw_rest[:]

        block = ctx.enter_context(nc.Block())

        @block.sync
        def _(sp):
            sp.dma_start(cst[:], const).then_inc(consts_in, 16)
            sp.dma_start(wgt[:], weights).then_inc(consts_in, 16)

            def load_item(c):
                if c >= 4:
                    sp.wait_ge(h_made, c - 3)
                sp.dma_start(itm[c % 4][:], item_t[:, c * CT * P:(c + 1) * CT * P]).then_inc(itm_full[c % 4], 16)

            def body(u, par):
                first = type(u) is int and u == 0
                if not (type(u) is int and u < 2):
                    sp.wait_ge(x1_ready, u - 1)
                sp.dma_start(xin[par][:], x_v[u]).then_inc(x_full[par], 16)
                for c in range(FULL):
                    if first:
                        load_item(c)
                    if not (first and c < RAW):
                        sp.wait_ge(lo_ready, u * CHUNKS + (c - RAW + 1))
                    row, at = c * CT // PER_ROW, c * CT % PER_ROW
                    sp.dma_start(raw[c % RAW][:], adj_main[u, row, :, at * U:(at + CT) * U]).then_inc(raw_full[c % RAW], 16)
                    if c == 10:
                        if first:
                            sp.wait_ge(zeroed, 1)
                        else:
                            sp.wait_ge(lo_ready, u * CHUNKS)
                        sp.dma_start(raw_rest[0:REST, :], adj_rest[u, :, :]).then_inc(rest_full, 16)
                    if c == 20 and not first:
                        sp.wait_ge(x1_ready, u)
                        sp.dma_start(out_v[u - 1], pay[:, :, 0:D]).then_inc(x1_stored, 16)
                    if first and c >= FULL - E:
                        if c == FULL - E:
                            sp.wait_ge(fill_set, 2)
                        sp.dma_start(slots_v[c - (FULL - E)], fill[:].rearrange("p (b w) -> p b w", w=W)).then_inc(filled, 16)

            blocks(sp, body)
            sp.wait_ge(x1_ready, NB)
            sp.dma_start(out_v[NB - 1], pay[:, :, 0:D]).then_inc(x1_stored, 16)
            sp.wait_ge(x1_stored, 16 * NB)

        @block.scalar
        def _(act):
            def h_high(c):
                act.wait_ge(h_made, c + 1)
                rows, n, at = (P, CT * D, c * CT * D) if c < FULL else (REST, D, KT * D)
                nc.scalar.activation(h_hi[0:rows, at:at + n], ps_h[c % 2][0:rows, 0:n], ACT.Copy).then_inc(hhi_ready, 1)

            def split_high(u, c):
                if c < FULL:
                    loads = (FULL - c % RAW - 1) // RAW + 1
                    act.wait_ge(raw_full[c % RAW], (u * loads + (c // RAW + 1)) * 16)
                else:
                    act.wait_ge(rest_full, (u + 1) * 16)
                if not (type(u) is int and u == 0 and c < SPLIT):
                    act.wait_ge(chunk_done, u * CHUNKS + (c - SPLIT + 1))
                nc.scalar.activation(a_hi[c % SPLIT][:, 0:tiles(c) * U], source(c), ACT.Copy).then_inc(hi_ready, 1)

            def relu(v, par):
                act.wait_ge(acc_ready, v + 1)
                if not (type(v) is int and v == 0):
                    act.wait_ge(relu_turned, v)
                nc.scalar.activation(rt[:], acc[par][:], ACT.Relu, bias=wgt[:, BUSER:BUSER + 1]).then_inc(relu_ready, 1)

            def std_1(u):
                act.wait_ge(mv1_ready, u + 1)
                nc.scalar.activation(std1[:], mv1[:, :, 1], ACT.Sqrt, bias=eps[0:TP, :]).then_inc(std1_ready, 1)

            def std_2(v):
                act.wait_ge(mv2_ready, v + 1)
                nc.scalar.activation(std2[:], mv2[:, :, 1], ACT.Sqrt, bias=eps[0:TP, :]).then_inc(std2_ready, 1)

            def copy_xn1t(u):
                act.wait_ge(xn1_turned, u + 1)
                if not (type(u) is int and u == 0):
                    act.wait_ge(acc_ready, u)
                nc.scalar.activation(xn1t[:], ps_x1[:], ACT.Copy).then_inc(xn1t_ready, 1)

            def copy_xn2t(v):
                act.wait_ge(xn2_turned, v + 1)
                if not (type(v) is int and v == 0):
                    act.wait_ge(logits_made, v)
                nc.scalar.activation(xn2t[:], ps_x2[:], ACT.Copy).then_inc(xn2t_ready, 1)

            def exp_(v):
                act.wait_ge(shifted_ready, v + 1)
                nc.scalar.activation(ex[:], logit[:], ACT.Exp).then_inc(exp_ready, 1)

            def body(u, par):
                first = type(u) is int and u == 0
                for c in range(CHUNKS):
                    split_high(u, c)
                    if first and c + AHEAD < CHUNKS:
                        h_high(c + AHEAD)
                    if c == 3 and not first:
                        relu(u - 1, 1 - par)
                    if c == 13:
                        std_1(u)
                        if not first:
                            std_2(u - 1)
                    if c == 21:
                        copy_xn1t(u)
                    if c == 23 and not first:
                        copy_xn2t(u - 1)
                    if c == 30 and not first:
                        exp_(u - 1)

            act.wait_ge(consts_in, 32)
            act.wait_ge(set_up, 1)
            h_high(0)
            h_high(1)
            blocks(act, body)
            relu(NB - 1, 1)
            std_2(NB - 1)
            copy_xn2t(NB - 1)
            exp_(NB - 1)

        @block.vector
        def _(dve):
            nc.vector.memset(raw_rest[:], 0.0).then_inc(zeroed, 1)
            nc.vector.memset(eps[:], EPS)
            nc.vector.memset(carry[:], 0.0)
            nc.vector.memset(h_hi[:, KT * D:].bitcast(f32), 0.0)
            nc.vector.memset(h_lo[:, KT * D:].bitcast(f32), 0.0).then_inc(set_up, 1)
            nc.vector.memset(fill[:], 0.0).then_inc(fill_set, 1)
            dve.wait_ge(fill_set, 1)
            nc.vector.memset(fill[:].bitcast(i32).rearrange("p (b w) -> p b w", w=W)[:, :, TOKEN], NOWHERE).then_inc(fill_set, 1)
            dve.wait_ge(consts_in, 32)
            nc.vector.tensor_copy(tok[:], cst[0:TP, TOK0:TOK0 + TJ])
            dve.wait_ge(set_up, 1)

            def h_low(c):
                dve.wait_ge(hhi_ready, c + 1)
                rows, n, at = (P, CT * D, c * CT * D) if c < FULL else (REST, D, KT * D)
                nc.vector.tensor_tensor(h_lo[0:rows, at:at + n], ps_h[c % 2][0:rows, 0:n],
                                        h_hi[0:rows, at:at + n].bitcast(f32), ALU.subtract).then_inc(hlo_ready, 1)

            def split_low(u, c):
                dve.wait_ge(hi_ready, u * CHUNKS + (c + 1))
                n = tiles(c) * U
                nc.vector.tensor_tensor(a_lo[c % SPLIT][:, 0:n], source(c), a_hi[c % SPLIT][:, 0:n].bitcast(f32),
                                        ALU.subtract).then_inc(lo_ready, 1)

            def stats_1(u, par):
                dve.wait_ge(x_full[par], (u + (2 - par)) * 8)
                for j in range(TJ):
                    last = nc.vector.bn_stats(st1[:, j, :], xin[par][:, j, :])
                last.then_inc(st1_ready, 1)
                wait_alone(dve, st1_ready, u + 1)
                for j in range(TJ):
                    last = nc.vector.bn_aggr(mv1[:, j, :], st1[:, j, :])
                last.then_inc(mv1_ready, 1)

            def norm_1(u, par):
                dve.wait_ge(std1_ready, u + 1)
                nc.vector.reciprocal(rstd1[:], std1[:]).then_inc(rstd1_ready, 1)
                dve.wait_ge(rstd1_ready, u + 1)
                if not (type(u) is int and u == 0):
                    dve.wait_ge(xn1_turned, u)
                for j in range(TJ):
                    last = nc.vector.tensor_scalar(xn1[:, j, :], xin[par][:, j, :], mv1[:, j, 0:1], rstd1[:, j:j + 1],
                                                   ALU.subtract, ALU.mult)
                last.then_inc(xn1_ready, 1)

            def add_x1(v, par):
                dve.wait_ge(relu_turned, v + 1)
                if not (type(v) is int and v == 0):
                    dve.wait_ge(scattered, v * (16 * TJ))
                    dve.wait_ge(x1_stored, v * 16)
                nc.vector.tensor_tensor(pay[:, :, 0:D], ps_r[:], xin[par][:], ALU.add).then_inc(x1_ready, 1)

            def stats_2(v):
                dve.wait_ge(x1_ready, v + 1)
                for j in range(TJ):
                    last = nc.vector.bn_stats(st2[:, j, :], pay[:, j, 0:D])
                last.then_inc(st2_ready, 1)
                wait_alone(dve, st2_ready, v + 1)
                for j in range(TJ):
                    last = nc.vector.bn_aggr(mv2[:, j, :], st2[:, j, :])
                last.then_inc(mv2_ready, 1)

            def norm_2(v):
                dve.wait_ge(std2_ready, v + 1)
                nc.vector.tensor_copy(pay[:, :, MEAN], mv2[:, :, 0])
                nc.vector.reciprocal(pay[:, :, RSTD], std2[:]).then_inc(rstd2_ready, 1)
                dve.wait_ge(rstd2_ready, v + 1)
                if not (type(v) is int and v == 0):
                    dve.wait_ge(xn2_turned, v)
                for j in range(TJ):
                    last = nc.vector.tensor_scalar(xn2[:, j, :], pay[:, j, 0:D], mv2[:, j, 0:1], pay[:, j, RSTD:RSTD + 1],
                                                   ALU.subtract, ALU.mult)
                last.then_inc(xn2_ready, 1)

            def wide(a):
                return a.unsqueeze(2).to_broadcast([TP, TJ, E])

            steps = [0]

            def step(v, instruction):
                steps[0] += 1
                instruction.then_inc(route, 1)
                dve.wait_ge(route, v * ROUTE_STEPS + steps[0])

            def gate_shift(v):
                steps[0] = 0
                dve.wait_ge(logits_made, v + 1)
                gateb = wgt[0:TP, GATEB:GATEB + TJ * E].rearrange("p (j e) -> p j e", e=E)
                step(v, nc.vector.tensor_tensor(logit[:], ps_l[:, 0:TJ * E].rearrange("p (j e) -> p j e", e=E), gateb, ALU.add))
                step(v, nc.vector.reduce_max(lmax[:], logit[:], AX))
                nc.vector.tensor_tensor(logit[:], logit[:], wide(lmax[:]), ALU.subtract).then_inc(shifted_ready, 1)

            def softmax(v):
                dve.wait_ge(exp_ready, v + 1)
                step(v, nc.vector.reduce_sum(esum[:], ex[:], AX))
                step(v, nc.vector.reciprocal(rsum[:], esum[:]))
                step(v, nc.vector.tensor_tensor(prob[:], ex[:], wide(rsum[:]), ALU.mult))
                step(v, nc.vector.reduce_max(pay[:, :, PROB], prob[:], AX))

            def choose(v):
                step(v, nc.vector.tensor_tensor(cand[:], prob[:], wide(pay[:, :, PROB]), ALU.is_equal))
                step(v, nc.vector.tensor_tensor(cand[:], cand[:], cst[0:TP, REV:REV + TJ * E].rearrange("p (j e) -> p j e", e=E), ALU.mult))
                step(v, nc.vector.reduce_max(cmax[:], cand[:], AX))

            def count_rows(v):
                step(v, nc.vector.tensor_tensor(onehot[:], cand[:], wide(cmax[:]), ALU.is_equal))
                nc.vector.reduce_sum(rowsum[:], onehot[:].rearrange("p j e -> p e j"), AX).then_inc(rowsum_ready, 1)

            def place(v):
                dve.wait_ge(counts_made, v + 1)
                step(v, nc.vector.tensor_tensor(before[:, 0, :], ps_l[:, 32:32 + E], carry[:], ALU.add))
                for j in range(1, TJ):
                    step(v, nc.vector.tensor_tensor(before[:, j, :], before[:, j - 1, :], onehot[:, j - 1, :], ALU.add))

            def address(v):
                nc.vector.tensor_tensor(carry[:], carry[:], ps_l[:, 40:40 + E], ALU.add)
                nc.vector.tensor_scalar(over[:], before[:], float(C), float(NOWHERE), ALU.is_ge, ALU.mult)
                step(v, nc.vector.tensor_tensor(where[:], before[:], cst[0:TP, EOFF:EOFF + TJ * E].rearrange("p (j e) -> p j e", e=E), ALU.add))
                step(v, nc.vector.tensor_tensor(where[:], where[:], over[:], ALU.add))

            def slots_of(v):
                nc.vector.tensor_copy(pay_i[:, :, TOKEN], tok[:])
                nc.vector.tensor_scalar(tok[:], tok[:], float(U), None, ALU.add)
                nc.vector.tensor_tensor(where[:], where[:], onehot[:], ALU.mult).then_inc(placed, 1)
                dve.wait_ge(placed, v + 1)
                nc.vector.reduce_sum(slot[:], where[:], AX).then_inc(summed, 1)
                dve.wait_ge(summed, v + 1)
                nc.vector.tensor_copy(slot_i[:], slot[:]).then_inc(slots_ready, 1)
                assert steps[0] == ROUTE_STEPS, steps[0]

            def body(u, par):
                first = type(u) is int and u == 0
                for c in range(CHUNKS):
                    split_low(u, c)
                    if first and c + AHEAD < CHUNKS:
                        h_low(c + AHEAD)
                    if c == 2:
                        stats_1(u, par)
                    if c == 15:
                        norm_1(u, par)
                    if not first:
                        if c == 8:
                            add_x1(u - 1, 1 - par)
                        if c == 10:
                            stats_2(u - 1)
                        if c == 17:
                            norm_2(u - 1)
                        if c == 27:
                            gate_shift(u - 1)
                        if c == 32:
                            softmax(u - 1)
                        if c == 33:
                            choose(u - 1)
                        if c == 34:
                            count_rows(u - 1)
                        if c == 37:
                            place(u - 1)
                        if c == 38:
                            address(u - 1)
                        if c == 39:
                            slots_of(u - 1)

            h_low(0)
            h_low(1)
            blocks(dve, body)
            add_x1(NB - 1, 1)
            stats_2(NB - 1)
            norm_2(NB - 1)
            gate_shift(NB - 1)
            softmax(NB - 1)
            choose(NB - 1)
            count_rows(NB - 1)
            place(NB - 1)
            address(NB - 1)
            slots_of(NB - 1)

        @block.tensor
        def _(pe):
            def make_h(c):
                if c < FULL:
                    pe.wait_ge(itm_full[c % 4], (c // 4 + 1) * 16)
                if c >= 2:
                    pe.wait_ge(hlo_ready, c - 1)
                for k in range(tiles(c)):
                    rows = P if c < FULL else REST
                    items = itm[c % 4][:, k * P:(k + 1) * P] if c < FULL else wgt[:, ITREST:ITREST + REST]
                    o = ps_h[c % 2][0:rows, k * D:(k + 1) * D]
                    nc.tensor.matmul(o, items, wgt[:, WIT:WIT + D], start=True, stop=False)
                    last = nc.tensor.matmul(o, cst[:, ONES:ONES + rows], wgt[:, BITEM:BITEM + D], start=False, stop=True)
                last.then_inc(h_made, 1)

            def products(u, par, c):
                if type(u) is int and u == 0:
                    pe.wait_ge(hlo_ready, c + 1)
                pe.wait_ge(lo_ready, u * CHUNKS + (c + 1))
                if c == 0 and not (type(u) is int and u < 2):
                    pe.wait_ge(relu_ready, u - 1)
                for k in range(tiles(c)):
                    t = c * CT + k
                    hi, lo = a_hi[c % SPLIT][:, k * U:(k + 1) * U], a_lo[c % SPLIT][:, k * U:(k + 1) * U]
                    wh, wl = h_hi[:, t * D:(t + 1) * D], h_lo[:, t * D:(t + 1) * D]
                    nc.tensor.matmul(acc[par][:], wh, hi, start=(t == 0), stop=False)
                    nc.tensor.matmul(acc[par][:], wh, lo, start=False, stop=False)
                    last = nc.tensor.matmul(acc[par][:], wl, hi, start=False, stop=False)
                last.then_inc(chunk_done, 1)

            def user_part(u, par):
                pe.wait_ge(xn1t_ready, u + 1)
                nc.tensor.matmul(acc[par][:], wgt[:, WUT:WUT + D], xn1t[:], start=False, stop=True).then_inc(acc_ready, 1)

            def turn_xn1(u):
                pe.wait_ge(xn1_ready, u + 1)
                for j in range(TJ):
                    last = nc.tensor.transpose(ps_x1[:, j * TP:(j + 1) * TP], xn1[:, j, :], ident[0:TP, 0:TP])
                last.then_inc(xn1_turned, 1)

            def turn_relu(v):
                pe.wait_ge(relu_ready, v + 1)
                for j in range(TJ):
                    last = nc.tensor.transpose(ps_r[:, j, :], rt[:, j * TP:(j + 1) * TP], ident)
                last.then_inc(relu_turned, 1)

            def turn_xn2(v):
                pe.wait_ge(xn2_ready, v + 1)
                for j in range(TJ):
                    last = nc.tensor.transpose(ps_x2[:, j * TP:(j + 1) * TP], xn2[:, j, :], ident[0:TP, 0:TP])
                last.then_inc(xn2_turned, 1)

            def logits(v):
                pe.wait_ge(xn2t_ready, v + 1)
                for j in range(TJ):
                    last = nc.tensor.matmul(ps_l[:, j * E:(j + 1) * E], xn2t[:, j * TP:(j + 1) * TP], wgt[:, GATEW:GATEW + E],
                                            start=True, stop=True)
                last.then_inc(logits_made, 1)

            def count(v):
                pe.wait_ge(rowsum_ready, v + 1)
                nc.tensor.matmul(ps_l[:, 32:32 + E], cst[0:TP, TRI:TRI + TP], rowsum[:], start=True, stop=True)
                nc.tensor.matmul(ps_l[:, 40:40 + E], cst[0:TP, ONES:ONES + TP], rowsum[:], start=True, stop=True).then_inc(counts_made, 1)

            def body(u, par):
                first = type(u) is int and u == 0
                for c in range(CHUNKS):
                    if first and c + AHEAD < CHUNKS:
                        make_h(c + AHEAD)
                    products(u, par, c)
                    if c == 17:
                        turn_xn1(u)
                    if not first:
                        if c == 5:
                            turn_relu(u - 1)
                        if c == 19:
                            turn_xn2(u - 1)
                        if c == 24:
                            logits(u - 1)
                        if c == 35:
                            count(u - 1)
                user_part(u, par)

            pe.wait_ge(consts_in, 32)
            make_h(0)
            make_h(1)
            blocks(pe, body)
            turn_relu(NB - 1)
            turn_xn2(NB - 1)
            logits(NB - 1)
            count(NB - 1)

        @block.gpsimd
        def _(pool):
            def scatter(v):
                wait_alone(pool, slots_ready, v + 1)
                for j in range(TJ):
                    nc.gpsimd.indirect_dma_start(slots, bass.IndirectOffsetOnAxis(ap=slot_i[:, j:j + 1], axis=0),
                                                 pay[:, j, :], None, bounds_check=E * CP - 1,
                                                 oob_is_err=False).then_inc(scattered, 16)

            pool.wait_ge(filled, 16 * E)
            with pool.Fori(0, NB) as v:
                scatter(v)
            pool.wait_ge(scattered, 16 * TJ * NB)

    def experts(ctx, cst, wgt):
        def sb(name, shape, dt=f32):
            return ctx.enter_context(nc.sbuf_tensor(name, shape, dt))

        def pb(name, shape):
            return ctx.enter_context(nc.psum_tensor(name, shape, f32))

        def sem(name):
            return ctx.enter_context(nc.semaphore(name))

        GC = max(GROUPS) * ROWS
        w1r = [sb(f"w1r{i}", [P, F]) for i in range(2)]
        w2r = [sb(f"w2r{i}", [P, FC, D]) for i in range(2)]
        w1h = [sb(f"w1h{i}", [P, F], f32r) for i in range(2)]
        w1l = [sb(f"w1l{i}", [P, F], f32r) for i in range(2)]
        w2h = [sb(f"w2h{i}", [P, FC, D], f32r) for i in range(2)]
        w2l = [sb(f"w2l{i}", [P, FC, D], f32r) for i in range(2)]
        natx = [sb(f"natx{i}", [ROWS, BLOCKS, W]) for i in range(2)]
        natr = [sb(f"natr{i}", [ROWS, BLOCKS, W]) for i in range(2)]
        xs = [sb(f"xs{i}", [ROWS, BLOCKS, D]) for i in range(2)]
        xh = [sb(f"xh{i}", [P, CP], f32r) for i in range(2)]
        xl = [sb(f"xl{i}", [P, CP], f32r) for i in range(2)]
        hr = [sb(f"hr{i}", [P, FC, GC]) for i in range(2)]
        hh = [sb(f"hh{i}", [P, FC, GC], f32r) for i in range(2)]
        hl = [sb(f"hl{i}", [P, FC, GC], f32r) for i in range(2)]
        yt = [sb(f"yt{i}", [P, GC]) for i in range(2)]
        shift = [sb(f"shift{i}", [ROWS, BLOCKS]) for i in range(2)]
        ysum = sb("ysum", [P, E * G])
        yzero = sb("yzero", [P, E * G])
        ybad = sb("ybad", [P, E * G])
        ybads = sb("ybads", [P, 1])
        res = [sb(f"res{i}", [ROWS, 4, D]) for i in range(2)]

        ps_1 = [pb(f"ps_1{i}", [P, GC]) for i in range(FC)]
        ps_x = pb("ps_x", [P, GC])
        ps_y = pb("ps_y", [P, GC])
        ps_o = [pb(f"ps_o{i}", [ROWS, 4, D]) for i in range(2)]

        w_full = [sem(f"w_full{i}") for i in range(2)]
        natx_full = [sem(f"natx_full{i}") for i in range(2)]
        natr_full = [sem(f"natr_full{i}") for i in range(2)]
        whi_ready, wlo_ready, xs_ready, x_turned = sem("whi_ready"), sem("wlo_ready"), sem("xs_ready"), sem("x_turned")
        xh_ready, xl_ready, up_made, relu_done = sem("xh_ready"), sem("xl_ready"), sem("up_made"), sem("relu_done")
        hh_ready, hl_ready, down_made, yt_ready = sem("hh_ready"), sem("hl_ready"), sem("down_made"), sem("yt_ready")
        y_turned, res_ready, shift_ready = sem("y_turned"), sem("res_ready"), sem("shift_ready")
        y_stored = [sem(f"y_stored{i}") for i in range(2)]
        flagging, bad_counted = sem("flagging"), sem("bad_counted")
        written = [sem(f"written{i}") for i in range(2)]
        ident = cst[:, IDENT:IDENT + P]

        def each(e, body):
            body(0, 0)
            with e.Fori(0, (E - 2) // 2) as i:
                body(i * 2 + 1, 1)
                body(i * 2 + 2, 0)
            body(E - 1, 1)

        def at(n, least):
            return not (type(n) is int and n < least)

        def of(e, par):
            return (e // 2 + 1) * 16 if type(e) is int else (e + (2 - par)) * 8

        def cols(g):
            return GFIRST[g] * ROWS, GROUPS[g] * ROWS

        def written_by(e, g, b):
            whole = 16 * sum(GROUPS[k] for k in range(b, G, 2))
            return e * whole + 16 * sum(GROUPS[k] for k in range(b, g, 2))

        block = ctx.enter_context(nc.Block())

        @block.sync
        def _(sp):
            def load_w(e, q):
                if at(e, 2):
                    sp.wait_ge(wlo_ready, e - 1)
                sp.dma_start(w1r[q][:], w1[e]).then_inc(w_full[q], 16)
                sp.dma_start(w2r[q][:], w2[e].rearrange("(f p) d -> p f d", p=P)).then_inc(w_full[q], 16)

            def load_x(e, q):
                if at(e, 2):
                    sp.wait_ge(xs_ready, e * G - G)
                sp.dma_start(natx[q][:], slots_v[e]).then_inc(natx_full[q], 16)

            def load_r(e, q):
                if at(e, 2):
                    sp.wait_ge(written[0], written_by(e - 1, 0, 0))
                    sp.wait_ge(written[1], written_by(e - 1, 0, 1))
                sp.dma_start(natr[q][:], slots_v[e]).then_inc(natr_full[q], 16)

            def body(e, q):
                if not (type(e) is int and e == E - 1):
                    load_x(e + 1, 1 - q)
                    load_w(e + 1, 1 - q)
                    load_r(e + 1, 1 - q)

            load_x(0, 0)
            load_w(0, 0)
            load_r(0, 0)
            each(sp, body)

        @block.scalar
        def _(act):
            def w_high(e, q):
                act.wait_ge(w_full[q], of(e, q) * 2)
                if at(e, 2):
                    act.wait_ge(down_made, e * G - G)
                nc.scalar.activation(w1h[q][:], w1r[q][:], ACT.Copy)
                nc.scalar.activation(w2h[q][:], w2r[q][:], ACT.Copy).then_inc(whi_ready, 1)

            def x_high(e, q, g):
                c0, n = cols(g)
                act.wait_ge(x_turned, e * G + (g + 1))
                if at(e, 2):
                    act.wait_ge(up_made, e * (G * FC) - G * FC)
                nc.scalar.activation(xh[q][:, c0:c0 + n], ps_x[:, 0:n], ACT.Copy).then_inc(xh_ready, 1)

            def relu(e, q, g):
                _, n = cols(g)
                if not (type(e) is int and e == 0 and g < 2):
                    act.wait_ge(hl_ready, e * G + (g - 1))
                for f in range(FC):
                    wait_alone(act, up_made, e * (G * FC) + (g * FC + f + 1))
                    nc.scalar.activation(hr[g % 2][:, f, 0:n], ps_1[f][:, 0:n], ACT.Relu,
                                         bias=b1_of(e, f)).then_inc(relu_done, 1)

            def y_out(e, g):
                _, n = cols(g)
                wait_alone(act, down_made, e * G + (g + 1))
                if not (type(e) is int and e == 0 and g < 2):
                    wait_alone(act, y_turned, e * G + (g - 1))
                    wait_alone(act, y_stored[g % 2], (e * 2 + g // 2) * 16)
                nc.scalar.activation(yt[g % 2][:, 0:n], ps_y[:, 0:n], ACT.Identity,
                                     bias=b2_of(e), accum_out=sum_of(e, g)).then_inc(yt_ready, 1)

            def store_y(e, g):
                c0, n = cols(g)
                act.wait_ge(yt_ready, e * G + (g + 1))
                act.dma_start(y_all[e, :, c0:c0 + n], yt[g % 2][:, 0:n]).then_inc(y_stored[g % 2], 16)

            def b1_of(e, f):
                o = e * FC + (B1 + f)
                return wgt[:, o:o + 1] if type(e) is int else wgt[:, bass.ds(o, 1)]

            def sum_of(e, g):
                o = e * G + g
                return ysum[:, o:o + 1] if type(e) is int else ysum[:, bass.ds(o, 1)]

            def normalise(e, q, g):
                if g == 0:
                    act.wait_ge(shift_ready, e + 1)
                    if at(e, 2):
                        act.wait_ge(x_turned, e * G - G)
                for k in range(GFIRST[g], GFIRST[g] + GROUPS[g]):
                    last = nc.scalar.activation(xs[q][:, k, :], natx[q][:, k, 0:D], ACT.Identity,
                                                scale=natx[q][:, k, RSTD:RSTD + 1], bias=shift[q][:, k:k + 1])
                last.then_inc(xs_ready, 1)

            def b2_of(e):
                o = e + B2
                return wgt[:, o:o + 1] if type(e) is int else wgt[:, bass.ds(o, 1)]

            def body(e, q):
                for g in range(G):
                    if not (type(e) is int and e == E - 1):
                        normalise(e + 1, 1 - q, g)
                    if g > 1:
                        store_y(e, g - 2)
                    elif not (type(e) is int and e == 0):
                        store_y(e - 1, G - 2 + g)
                    relu(e, q, g)
                    if not (type(e) is int and e == E - 1):
                        x_high(e + 1, 1 - q, g)
                        if g == 2:
                            w_high(e + 1, 1 - q)
                    if g > 0:
                        y_out(e, g - 1)
                    elif not (type(e) is int and e == 0):
                        y_out(e - 1, G - 1)

            w_high(0, 0)
            for g in range(G):
                normalise(0, 0, g)
            for g in range(G):
                x_high(0, 0, g)
            each(act, body)
            y_out(E - 1, G - 1)
            store_y(E - 1, G - 2)
            store_y(E - 1, G - 1)
            for b in range(2):
                act.wait_ge(y_stored[b], 16 * E * G // 2)

        @block.vector
        def _(dve):
            def w_low(e, q):
                dve.wait_ge(whi_ready, e + 1)
                nc.vector.tensor_tensor(w1l[q][:], w1r[q][:], w1h[q][:].bitcast(f32), ALU.subtract)
                nc.vector.tensor_tensor(w2l[q][:], w2r[q][:], w2h[q][:].bitcast(f32), ALU.subtract).then_inc(wlo_ready, 1)

            def x_low(e, q, g):
                c0, n = cols(g)
                dve.wait_ge(xh_ready, e * G + (g + 1))
                nc.vector.tensor_tensor(xl[q][:, c0:c0 + n], ps_x[:, 0:n], xh[q][:, c0:c0 + n].bitcast(f32),
                                        ALU.subtract).then_inc(xl_ready, 1)

            def split_h(e, g):
                _, n = cols(g)
                b = g % 2
                dve.wait_ge(relu_done, e * (G * FC) + (g + 1) * FC)
                if not (type(e) is int and e == 0 and g < 2):
                    dve.wait_ge(down_made, e * G + (g - 1))
                nc.vector.tensor_copy(hh[b][:, :, 0:n], hr[b][:, :, 0:n]).then_inc(hh_ready, 1)
                dve.wait_ge(hh_ready, e * G + (g + 1))
                nc.vector.tensor_tensor(hl[b][:, :, 0:n], hr[b][:, :, 0:n], hh[b][:, :, 0:n].bitcast(f32),
                                        ALU.subtract).then_inc(hl_ready, 1)

            def shifts(e, q):
                dve.wait_ge(natx_full[q], of(e, q))
                if at(e, 2):
                    dve.wait_ge(xs_ready, e * G - G)
                nc.vector.scalar_tensor_tensor(out=shift[q][:], in0=natx[q][:, :, MEAN], scalar=-1.0, in1=natx[q][:, :, RSTD],
                                               op0=ALU.mult, op1=ALU.mult).then_inc(shift_ready, 1)

            def result(e, q, g):
                b = g % 2
                if g == 0:
                    dve.wait_ge(natr_full[q], of(e, q))
                dve.wait_ge(y_turned, e * G + (g + 1))
                if not (type(e) is int and e == 0 and g < 2):
                    dve.wait_ge(written[b], written_by(e, g, b))
                for k in range(GROUPS[g]):
                    row = natr[q][:, GFIRST[g] + k, :]
                    last = nc.vector.scalar_tensor_tensor(out=res[b][:, k, :], in0=ps_o[b][:, k, :], scalar=row[:, PROB:PROB + 1],
                                                          in1=row[:, 0:D], op0=ALU.mult, op1=ALU.add)
                last.then_inc(res_ready, 1)

            def body(e, q):
                if not (type(e) is int and e == E - 1):
                    shifts(e + 1, 1 - q)
                for g in range(G):
                    split_h(e, g)
                    if not (type(e) is int and e == E - 1):
                        x_low(e + 1, 1 - q, g)
                        if g == 2:
                            w_low(e + 1, 1 - q)
                    if g > 1:
                        result(e, q, g - 2)
                    elif not (type(e) is int and e == 0):
                        result(e - 1, 1 - q, G - 2 + g)

            shifts(0, 0)
            w_low(0, 0)
            for g in range(G):
                x_low(0, 0, g)
            each(dve, body)
            result(E - 1, 1, G - 2)
            result(E - 1, 1, G - 1)
            dve.wait_ge(yt_ready, E * G)
            nc.vector.tensor_scalar(yzero[:], ysum[:], 0.0, None, ALU.mult).then_inc(flagging, 1)
            dve.wait_ge(flagging, 1)
            nc.vector.tensor_scalar(ybad[:], yzero[:], 0.0, None, ALU.not_equal).then_inc(flagging, 1)
            dve.wait_ge(flagging, 2)
            nc.vector.reduce_sum(ybads[:], ybad[:], AX).then_inc(flagging, 1)
            dve.wait_ge(bad_counted, 1)
            nc.vector.tensor_copy(not_finite[:], ps_x[0:1, 0:1]).then_inc(flagging, 1)

        @block.tensor
        def _(pe):
            def turn_x(e, q, g):
                pe.wait_ge(xs_ready, e * G + (g + 1))
                if not (type(e) is int and e == 0 and g == 0):
                    pe.wait_ge(xl_ready, e * G + g)
                for k in range(GROUPS[g]):
                    last = nc.tensor.transpose(ps_x[:, k * ROWS:(k + 1) * ROWS], xs[q][:, GFIRST[g] + k, :],
                                               ident[0:ROWS, 0:ROWS])
                last.then_inc(x_turned, 1)

            def up(e, q, g):
                c0, n = cols(g)
                if g == 0:
                    pe.wait_ge(wlo_ready, e + 1)
                pe.wait_ge(xl_ready, e * G + (g + 1))
                for f in range(FC):
                    if not (type(e) is int and e == 0 and g == 0):
                        pe.wait_ge(relu_done, e * (G * FC) + ((g - 1) * FC + f + 1))
                    wh, wl = w1h[q][:, f * P:(f + 1) * P], w1l[q][:, f * P:(f + 1) * P]
                    o = ps_1[f][:, 0:n]
                    nc.tensor.matmul(o, wh, xh[q][:, c0:c0 + n], start=True, stop=False)
                    nc.tensor.matmul(o, wh, xl[q][:, c0:c0 + n], start=False, stop=False)
                    nc.tensor.matmul(o, wl, xh[q][:, c0:c0 + n], start=False, stop=True).then_inc(up_made, 1)

            def down(e, q, g):
                _, n = cols(g)
                b = g % 2
                pe.wait_ge(hl_ready, e * G + (g + 1))
                if not (type(e) is int and e == 0 and g == 0):
                    pe.wait_ge(yt_ready, e * G + g)
                for f in range(FC):
                    o = ps_y[:, 0:n]
                    hi, lo = hh[b][:, f, 0:n], hl[b][:, f, 0:n]
                    nc.tensor.matmul(o, w2h[q][:, f, :], hi, start=(f == 0), stop=False)
                    nc.tensor.matmul(o, w2h[q][:, f, :], lo, start=False, stop=False)
                    last = nc.tensor.matmul(o, w2l[q][:, f, :], hi, start=False, stop=(f == FC - 1))
                last.then_inc(down_made, 1)

            def turn_y(e, g):
                b = g % 2
                pe.wait_ge(yt_ready, e * G + (g + 1))
                if not (type(e) is int and e == 0 and g < 2):
                    pe.wait_ge(res_ready, e * G + (g - 1))
                for k in range(GROUPS[g]):
                    last = nc.tensor.transpose(ps_o[b][:, k, :], yt[b][:, k * ROWS:(k + 1) * ROWS], ident)
                last.then_inc(y_turned, 1)

            def body(e, q):
                for g in range(G):
                    up(e, q, g)
                    if not (type(e) is int and e == E - 1):
                        turn_x(e + 1, 1 - q, g)
                    if g > 0:
                        down(e, q, g - 1)
                    elif not (type(e) is int and e == 0):
                        down(e - 1, 1 - q, G - 1)
                    if g > 1:
                        turn_y(e, g - 2)
                    elif not (type(e) is int and e == 0):
                        turn_y(e - 1, G - 2 + g)

            for g in range(G):
                turn_x(0, 0, g)
            each(pe, body)
            down(E - 1, 1, G - 1)
            turn_y(E - 1, G - 2)
            turn_y(E - 1, G - 1)
            pe.wait_ge(flagging, 3)
            nc.tensor.matmul(ps_x[0:1, 0:1], ybads[:], cst[:, ONES:ONES + 1], start=True, stop=True).then_inc(bad_counted, 1)

        @block.gpsimd
        def _(pool):
            def write(e, q, g):
                wait_alone(pool, res_ready, e * G + (g + 1))
                for k in range(GROUPS[g]):
                    token = natr[q][:].bitcast(i32)[:, GFIRST[g] + k, TOKEN:TOKEN + 1]
                    nc.gpsimd.indirect_dma_start(out, bass.IndirectOffsetOnAxis(ap=token, axis=0), res[g % 2][:, k, :], None,
                                                 bounds_check=T - 1, oob_is_err=False).then_inc(written[g % 2], 16)

            def body(e, q):
                for g in range(G):
                    if g > 1:
                        write(e, q, g - 2)
                    elif not (type(e) is int and e == 0):
                        write(e - 1, 1 - q, G - 2 + g)

            each(pool, body)
            write(E - 1, 1, G - 2)
            write(E - 1, 1, G - 1)
            for b in range(2):
                pool.wait_ge(written[b], written_by(E, 0, b))

    def guard(ctx, cst):
        def sb(name, shape, dt=f32):
            return ctx.enter_context(nc.sbuf_tensor(name, shape, dt))

        yb = sb("yb", [P, ROWS])
        row = sb("row", [ROWS, W])
        y = sb("y", [ROWS, D])
        above = sb("above", [ROWS, D])
        below = sb("below", [ROWS, D])
        less = sb("less", [ROWS, D])
        finite = sb("finite", [ROWS, D], i32)
        fixed = sb("fixed", [ROWS, D])
        ps = ctx.enter_context(nc.psum_tensor("ps", [ROWS, D], f32))
        loaded, turned, guarding, rewritten, block_free = [
            ctx.enter_context(nc.semaphore(n)) for n in ("loaded", "turned", "guarding", "rewritten", "block_free")]
        STEPS = 5

        def every(engine, body):
            flag = engine.value_load(not_finite[0:1, 0:1])
            with engine.If(flag > 0):
                with engine.Fori(0, E) as e:
                    with engine.Fori(0, BLOCKS) as b:
                        body(e, b, e * BLOCKS + (b + 1))

        block = ctx.enter_context(nc.Block())

        @block.sync
        def _(sp):
            def body(e, b, k):
                sp.wait_ge(block_free, k)
                sp.dma_start(yb[:], y_all[e, :, bass.ds(b * ROWS, ROWS)]).then_inc(loaded, 16)
                sp.dma_start(row[:], slots_b[e, b]).then_inc(loaded, 16)
            every(sp, body)

        @block.tensor
        def _(pe):
            def body(e, b, k):
                pe.wait_ge(loaded, k * 32)
                nc.tensor.transpose(ps[:], yb[:], cst[:, IDENT:IDENT + P]).then_inc(turned, 1)
            every(pe, body)

        @block.vector
        def _(dve):
            def body(e, b, k):
                def step(i, instruction):
                    instruction.then_inc(guarding, 1)
                    wait_alone(dve, guarding, k * STEPS + (i - STEPS))

                wait_alone(dve, turned, k)
                step(1, nc.vector.tensor_scalar(y[:], ps[:], row[:, PROB:PROB + 1], None, ALU.mult))
                nc.vector.tensor_scalar(above[:], y[:], 0.0, 1e4, ALU.is_gt, ALU.mult)
                nc.vector.tensor_scalar(below[:], y[:], 0.0, 1e4, ALU.is_lt, ALU.mult)
                step(2, nc.vector.tensor_tensor(less[:], y[:], y[:], ALU.subtract))
                nc.vector.tensor_scalar(finite[:], less[:], 0.0, None, ALU.is_equal)
                step(3, nc.vector.tensor_tensor(fixed[:], above[:], below[:], ALU.subtract))
                step(4, nc.vector.copy_predicated(fixed[:], finite[:], y[:]))
                step(5, nc.vector.tensor_tensor(fixed[:], fixed[:], row[:, 0:D], ALU.add))
            every(dve, body)

        @block.gpsimd
        def _(pool):
            pool.sem_inc(block_free, 1)

            def body(e, b, k):
                wait_alone(pool, guarding, k * STEPS)
                nc.gpsimd.indirect_dma_start(out, bass.IndirectOffsetOnAxis(ap=row[:].bitcast(i32)[:, TOKEN:TOKEN + 1], axis=0),
                                             fixed[:], None, bounds_check=T - 1, oob_is_err=False).then_inc(rewritten, 16)
                wait_alone(pool, rewritten, k * 16)
                pool.sem_inc(block_free, 1)
            every(pool, body)

    with ExitStack() as ctx:
        not_finite = ctx.enter_context(nc.sbuf_tensor("not_finite", [1, 1], i32))
        consts_in = ctx.enter_context(nc.semaphore("consts_in"))
        cst = ctx.enter_context(nc.sbuf_tensor("cst", [P, CONST_W], f32))
        wgt = ctx.enter_context(nc.sbuf_tensor("wgt", [P, WEIGHT_W], f32))
        with ExitStack() as inner:
            stream(inner, cst, wgt)
        with ExitStack() as inner:
            experts(inner, cst, wgt)
        with ExitStack() as inner:
            guard(inner, cst)


def kernel(x, adj, L0_gnn_item_feat, L0_gnn_W_item, L0_gnn_b_item, L0_gnn_W_user, L0_gnn_b_user,
           L0_ffn_gate_w, L0_ffn_gate_b, L0_ffn_w1, L0_ffn_b1, L0_ffn_w2, L0_ffn_b2):
    import numpy as np
    import concourse.bacc as bacc
    from concourse.bass_utils import run_bass_kernel_spmd

    f = np.float32
    a = np.asarray(adj).reshape(NB, TP, TJ, N)
    main = np.empty((NB, KT // PER_ROW, P, PER_ROW, TJ, TP), f)
    for u in range(NB):
        t = np.ascontiguousarray(a[u].transpose(2, 1, 0))
        main[u] = t[:KT * P].reshape(KT // PER_ROW, PER_ROW, P, TJ, TP).transpose(0, 2, 1, 3, 4)
    rest = np.ascontiguousarray(a[:, :, :, KT * P:].transpose(0, 3, 2, 1)).reshape(NB, REST, U)
    item_t = np.ascontiguousarray(np.asarray(L0_gnn_item_feat).T)

    const = np.zeros((P, CONST_W), f)
    const[:, IDENT:IDENT + P] = np.eye(P)
    const[:, TRI:TRI + P] = np.triu(np.ones((P, P)), 1)
    const[:, ONES:ONES + P] = 1.0
    const[:, REV:REV + TJ * E] = np.tile(np.arange(E, 0, -1), TJ)
    const[:, EOFF:EOFF + TJ * E] = np.tile(np.arange(E) * CP, TJ)
    const[:, TOK0:TOK0 + TJ] = np.arange(P)[:, None] * TJ + np.arange(TJ)

    weights = np.zeros((P, WEIGHT_W), f)
    weights[:, WIT:WIT + D] = np.asarray(L0_gnn_W_item).T
    weights[:, WUT:WUT + D] = np.asarray(L0_gnn_W_user).T
    weights[0, BITEM:BITEM + D] = L0_gnn_b_item
    weights[:, ITREST:ITREST + REST] = item_t[:, KT * P:]
    weights[:, GATEW:GATEW + E] = L0_ffn_gate_w
    weights[:, GATEB:GATEB + TJ * E] = np.tile(np.asarray(L0_ffn_gate_b), TJ)
    weights[:, BUSER] = L0_gnn_b_user
    weights[:, B1:B1 + E * FC] = np.asarray(L0_ffn_b1).reshape(E * FC, P).T
    weights[:, B2:B2 + E] = np.asarray(L0_ffn_b2).T

    arrays = {
        "adj_main": main.reshape(NB, KT // PER_ROW, P, PER_ROW * U), "adj_rest": rest, "x_in": np.ascontiguousarray(x),
        "item_t": item_t, "const": const, "weights": weights,
        "w1_in": np.ascontiguousarray(L0_ffn_w1), "w2_in": np.ascontiguousarray(L0_ffn_w2),
    }
    nc = bacc.Bacc("TRN2", target_bir_lowering=False, num_devices=1)
    args = [nc.dram_tensor(k, v.shape, mybir.dt.from_np(v.dtype), kind="ExternalInput").ap() for k, v in arrays.items()]
    out = nc.dram_tensor("out", (T, D), mybir.dt.float32, kind="ExternalOutput").ap()
    build(nc, *args, out)
    return run_bass_kernel_spmd(nc, [arrays], core_ids=[0]).results[0]["out"]
```

```python
import concourse.bass as bass
from concourse import mybir
from contextlib import ExitStack

P = 128
T = 10000
N = 10000
D = 128
E = 8
F = 512
FC = F // P
C = 1563
EPS = 1e-5

U = 500
NB = T // U
TP = 125
TJ = U // TP
KT = N // P
REST = N - KT * P
CT = 2
FULL = KT // CT
CHUNKS = FULL + 1
PER_ROW = 26
RAW = 10
SPLIT = 5
AHEAD = 2

ROWS = 112
BLOCKS = 14
CP = ROWS * BLOCKS
GROUPS = [4, 4, 3, 3]
GFIRST = [0, 4, 8, 11]
G = len(GROUPS)
LEAD = 2
DOWN_LAG = 2
STORE_LAG = 3
W = 132
MEAN, RSTD, PROB, TOKEN = 128, 129, 130, 131
NOWHERE = 1 << 20

IDENT, TRI, ONES, REV, EOFF, TOK0, CONST_W = 0, 128, 256, 384, 416, 448, 452
WIT, WUT, BITEM, ITREST, GATEW, GATEB, BUSER, B1, B2, WEIGHT_W = 0, 128, 256, 384, 400, 408, 440, 441, 473, 481


def build(nc, adj_main, adj_rest, x, item_t, const, weights, w1, w2, out):
    f32, f32r, i32 = mybir.dt.float32, mybir.dt.float32r, mybir.dt.int32
    ALU, ACT, AX = mybir.AluOpType, mybir.ActivationFunctionType, mybir.AxisListType.X

    slots = nc.dram_tensor("slots", (E * CP, W), f32, kind="Internal").ap()
    x_v = x.rearrange("(u p j) d -> u p j d", p=TP, j=TJ)
    out_v = out.rearrange("(u p j) d -> u p j d", p=TP, j=TJ)
    slots_v = slots.rearrange("(e p b) w -> e p b w", e=E, p=ROWS)
    slots_b = slots.rearrange("(e p b) w -> e b p w", e=E, p=ROWS)
    y_all = nc.dram_tensor("y_all", (E, P, CP), f32, kind="Internal").ap()

    def wait_alone(engine, semaphore, value):
        if type(value) is not int:
            engine.compute_val(value)
        engine.wait_ge(consts_in, 32)
        engine.wait_ge(semaphore, value)

    def stream(ctx, cst, wgt):
        def sb(name, shape, dt=f32):
            return ctx.enter_context(nc.sbuf_tensor(name, shape, dt))

        def pb(name, shape):
            return ctx.enter_context(nc.psum_tensor(name, shape, f32))

        def sem(name):
            return ctx.enter_context(nc.semaphore(name))

        h_hi = sb("h_hi", [P, (KT + 1) * D], f32r)
        h_lo = sb("h_lo", [P, (KT + 1) * D], f32r)
        raw = [sb(f"raw{i}", [P, CT * U]) for i in range(RAW)]
        raw_rest = sb("raw_rest", [P, U])
        a_hi = [sb(f"a_hi{i}", [P, CT * U], f32r) for i in range(SPLIT)]
        a_lo = [sb(f"a_lo{i}", [P, CT * U], f32r) for i in range(SPLIT)]
        itm = [sb(f"itm{i}", [P, CT * P]) for i in range(4)]
        fill = sb("fill", [ROWS, W])
        xin = [sb(f"xin{i}", [TP, TJ, D]) for i in range(2)]
        pay = sb("pay", [TP, TJ, W])
        pay_i = pay[:].bitcast(i32)
        st1 = sb("st1", [TP, TJ, 6])
        st2 = sb("st2", [TP, TJ, 6])
        mv1 = sb("mv1", [TP, TJ, 2])
        mv2 = sb("mv2", [TP, TJ, 2])
        std1 = sb("std1", [TP, TJ])
        std2 = sb("std2", [TP, TJ])
        rstd1 = sb("rstd1", [TP, TJ])
        xn1 = sb("xn1", [TP, TJ, D])
        xn2 = sb("xn2", [TP, TJ, D])
        xn1t = sb("xn1t", [P, U])
        xn2t = sb("xn2t", [P, U])
        rt = sb("rt", [P, U])
        eps = sb("eps", [P, 1])
        logit = sb("logit", [TP, TJ, E])
        lmax = sb("lmax", [TP, TJ])
        ex = sb("ex", [TP, TJ, E])
        esum = sb("esum", [TP, TJ])
        rsum = sb("rsum", [TP, TJ])
        prob = sb("prob", [TP, TJ, E])
        cand = sb("cand", [TP, TJ, E])
        cmax = sb("cmax", [TP, TJ])
        onehot = sb("onehot", [TP, TJ, E])
        rowsum = sb("rowsum", [TP, E])
        carry = sb("carry", [TP, E])
        before = sb("before", [TP, TJ, E])
        over = sb("over", [TP, TJ, E])
        where = sb("where", [TP, TJ, E])
        slot = sb("slot", [TP, TJ])
        slot_i = sb("slot_i", [TP, TJ], i32)
        tok = sb("tok", [TP, TJ])
        most = sb("most", [TP, 1])
        most_i = sb("most_i", [TP, 1], i32)

        acc = [pb(f"acc{i}", [P, U]) for i in range(2)]
        ps_r = pb("ps_r", [TP, TJ, D])
        ps_x1 = pb("ps_x1", [P, U])
        ps_x2 = pb("ps_x2", [P, U])
        ps_l = pb("ps_l", [TP, 64])
        ps_h = [pb(f"ps_h{i}", [P, CT * D]) for i in range(2)]

        zeroed, filled, fill_set = sem("zeroed"), sem("filled"), sem("fill_set")
        raw_full = [sem(f"raw_full{i}") for i in range(RAW)]
        rest_full = sem("rest_full")
        itm_full = [sem(f"itm_full{i}") for i in range(4)]
        x_full = [sem(f"x_full{i}") for i in range(2)]
        hi_ready, lo_ready, chunk_done, user_added = sem("hi_ready"), sem("lo_ready"), sem("chunk_done"), sem("user_added")
        h_made, hhi_ready, hlo_ready = sem("h_made"), sem("hhi_ready"), sem("hlo_ready")
        st1_ready, mv1_ready, std1_ready, rstd1_ready = sem("st1_ready"), sem("mv1_ready"), sem("std1_ready"), sem("rstd1_ready")
        xn1_ready, xn1_turned, xn1t_ready = sem("xn1_ready"), sem("xn1_turned"), sem("xn1t_ready")
        relu_ready, relu_turned, x1_ready, x1_stored = sem("relu_ready"), sem("relu_turned"), sem("x1_ready"), sem("x1_stored")
        st2_ready, mv2_ready, std2_ready, rstd2_ready = sem("st2_ready"), sem("mv2_ready"), sem("std2_ready"), sem("rstd2_ready")
        xn2_ready, xn2_turned, xn2t_ready, logits_made = sem("xn2_ready"), sem("xn2_turned"), sem("xn2t_ready"), sem("logits_made")
        route = sem("route")
        shifted_ready, exp_ready, rowsum_ready, counts_made = sem("shifted_ready"), sem("exp_ready"), sem("rowsum_ready"), sem("counts_made")
        slots_ready, scattered = sem("slots_ready"), sem("scattered")
        most_ready = sem("most_ready")
        placed, summed, set_up = sem("placed"), sem("summed"), sem("set_up")
        ROUTE_STEPS = 16

        ident = cst[:, IDENT:IDENT + P]

        def blocks(e, body):
            body(0, 0)
            body(1, 1)
            with e.Fori(1, NB // 2) as i:
                body(i * 2, 0)
                body(i * 2 + 1, 1)

        def tiles(c):
            return CT if c < FULL else 1

        def source(c):
            return raw[c % RAW][:] if c < FULL else raw_rest[:]

        block = ctx.enter_context(nc.Block())

        @block.sync
        def _(sp):
            sp.dma_start(cst[:], const).then_inc(consts_in, 16)
            sp.dma_start(wgt[:], weights).then_inc(consts_in, 16)

            def load_item(c):
                if c >= 4:
                    sp.wait_ge(h_made, c - 3)
                sp.dma_start(itm[c % 4][:], item_t[:, c * CT * P:(c + 1) * CT * P]).then_inc(itm_full[c % 4], 16)

            def body(u, par):
                first = type(u) is int and u == 0
                if not (type(u) is int and u < 2):
                    sp.wait_ge(x1_ready, u - 1)
                sp.dma_start(xin[par][:], x_v[u]).then_inc(x_full[par], 16)
                for c in range(FULL):
                    if first:
                        load_item(c)
                    if not (first and c < RAW):
                        sp.wait_ge(lo_ready, u * CHUNKS + (c - RAW + 1))
                    row, at = c * CT // PER_ROW, c * CT % PER_ROW
                    sp.dma_start(raw[c % RAW][:], adj_main[u, row, :, at * U:(at + CT) * U]).then_inc(raw_full[c % RAW], 16)
                    if c == 10:
                        if first:
                            sp.wait_ge(zeroed, 1)
                        else:
                            sp.wait_ge(lo_ready, u * CHUNKS)
                        sp.dma_start(raw_rest[0:REST, :], adj_rest[u, :, :]).then_inc(rest_full, 16)
                    if c == 6 and not (type(u) is int and u < 2):
                        store_x1(u - 2)
                    if first and c % 4 == 3 and c // 4 < E:
                        if c == 3:
                            sp.wait_ge(fill_set, 2)
                        sp.dma_start(slots_v[c // 4], fill[:].unsqueeze(1).to_broadcast([ROWS, BLOCKS, W])).then_inc(filled, 16)

            def store_x1(v):
                wait_alone(sp, most_ready, v + 1)
                sp.wait_ge(consts_in, 32)
                most = sp.value_load(most_i[0:1, 0:1])
                with sp.If(most > C):
                    sp.dma_start(out_v[v], pay[:, :, 0:D]).then_inc(x1_stored, 16)
                with sp.Else():
                    sp.sem_inc(x1_stored, 16)

            blocks(sp, body)
            sp.dma_start(w1r_0[:], w1[0]).then_inc(w_first, 16)
            sp.dma_start(w2r_0[:], w2[0].rearrange("(f p) d -> p f d", p=P)).then_inc(w_first, 16)
            store_x1(NB - 2)
            store_x1(NB - 1)
            sp.wait_ge(x1_stored, 16 * NB)
            sp.wait_ge(w_first, 32)

        @block.scalar
        def _(act):
            def h_high(c):
                act.wait_ge(h_made, c + 1)
                rows, n, at = (P, CT * D, c * CT * D) if c < FULL else (REST, D, KT * D)
                nc.scalar.activation(h_hi[0:rows, at:at + n], ps_h[c % 2][0:rows, 0:n], ACT.Copy).then_inc(hhi_ready, 1)

            def split_high(u, c):
                if c < FULL:
                    loads = (FULL - c % RAW - 1) // RAW + 1
                    act.wait_ge(raw_full[c % RAW], (u * loads + (c // RAW + 1)) * 16)
                else:
                    act.wait_ge(rest_full, (u + 1) * 16)
                if not (type(u) is int and u == 0 and c < SPLIT):
                    act.wait_ge(chunk_done, u * CHUNKS + (c - SPLIT + 1))
                nc.scalar.activation(a_hi[c % SPLIT][:, 0:tiles(c) * U], source(c), ACT.Copy).then_inc(hi_ready, 1)

            def relu(v, par):
                act.wait_ge(chunk_done, (v + 1) * CHUNKS)
                if not (type(v) is int and v == 0):
                    act.wait_ge(relu_turned, v)
                nc.scalar.activation(rt[:], acc[par][:], ACT.Relu, bias=wgt[:, BUSER:BUSER + 1]).then_inc(relu_ready, 1)

            def std_1(u):
                act.wait_ge(mv1_ready, u + 1)
                nc.scalar.activation(std1[:], mv1[:, :, 1], ACT.Sqrt, bias=eps[0:TP, :]).then_inc(std1_ready, 1)

            def std_2(v):
                act.wait_ge(mv2_ready, v + 1)
                nc.scalar.activation(std2[:], mv2[:, :, 1], ACT.Sqrt, bias=eps[0:TP, :]).then_inc(std2_ready, 1)

            def copy_xn1t(u):
                act.wait_ge(xn1_turned, u + 1)
                if not (type(u) is int and u == 0):
                    act.wait_ge(user_added, u)
                nc.scalar.activation(xn1t[:], ps_x1[:], ACT.Copy).then_inc(xn1t_ready, 1)

            def copy_xn2t(v):
                act.wait_ge(xn2_turned, v + 1)
                if not (type(v) is int and v == 0):
                    act.wait_ge(logits_made, v)
                nc.scalar.activation(xn2t[:], ps_x2[:], ACT.Copy).then_inc(xn2t_ready, 1)

            def exp_(v):
                act.wait_ge(shifted_ready, v + 1)
                nc.scalar.activation(ex[:], logit[:], ACT.Exp).then_inc(exp_ready, 1)

            def body(u, par):
                first = type(u) is int and u == 0
                for c in range(CHUNKS):
                    split_high(u, c)
                    if first and c + 1 < CHUNKS:
                        h_high(c + 1)
                    if c == 3 and not first:
                        relu(u - 1, 1 - par)
                    if c == 13:
                        std_1(u)
                        if not first:
                            std_2(u - 1)
                    if c == 23:
                        copy_xn1t(u)
                    if c == 20 and not first:
                        copy_xn2t(u - 1)
                    if c == 26 and not first:
                        exp_(u - 1)

            act.wait_ge(consts_in, 32)
            act.wait_ge(set_up, 1)
            h_high(0)
            blocks(act, body)
            relu(NB - 1, 1)
            std_2(NB - 1)
            copy_xn2t(NB - 1)
            exp_(NB - 1)

        @block.vector
        def _(dve):
            nc.vector.memset(raw_rest[:], 0.0).then_inc(zeroed, 1)
            nc.vector.memset(eps[:], EPS)
            nc.vector.memset(carry[:], 0.0)
            nc.vector.memset(h_hi[:, KT * D:].bitcast(f32), 0.0)
            nc.vector.memset(h_lo[:, KT * D:].bitcast(f32), 0.0).then_inc(set_up, 1)
            nc.vector.memset(fill[:], 0.0).then_inc(fill_set, 1)
            dve.wait_ge(fill_set, 1)
            nc.vector.memset(fill[:, TOKEN:TOKEN + 1].bitcast(i32), NOWHERE).then_inc(fill_set, 1)
            dve.wait_ge(consts_in, 32)
            nc.vector.tensor_copy(tok[:], cst[0:TP, TOK0:TOK0 + TJ])
            dve.wait_ge(set_up, 1)

            def h_low(c):
                dve.wait_ge(hhi_ready, c + 1)
                rows, n, at = (P, CT * D, c * CT * D) if c < FULL else (REST, D, KT * D)
                nc.vector.tensor_tensor(h_lo[0:rows, at:at + n], ps_h[c % 2][0:rows, 0:n],
                                        h_hi[0:rows, at:at + n].bitcast(f32), ALU.subtract).then_inc(hlo_ready, 1)

            def split_low(u, c):
                dve.wait_ge(hi_ready, u * CHUNKS + (c + 1))
                n = tiles(c) * U
                nc.vector.tensor_tensor(a_lo[c % SPLIT][:, 0:n], source(c), a_hi[c % SPLIT][:, 0:n].bitcast(f32),
                                        ALU.subtract).then_inc(lo_ready, 1)

            def stats_1(u, par):
                dve.wait_ge(x_full[par], (u + (2 - par)) * 8)
                for j in range(TJ):
                    last = nc.vector.bn_stats(st1[:, j, :], xin[par][:, j, :])
                last.then_inc(st1_ready, 1)
                wait_alone(dve, st1_ready, u + 1)
                for j in range(TJ):
                    last = nc.vector.bn_aggr(mv1[:, j, :], st1[:, j, :])
                last.then_inc(mv1_ready, 1)

            def norm_1(u, par):
                dve.wait_ge(std1_ready, u + 1)
                nc.vector.reciprocal(rstd1[:], std1[:]).then_inc(rstd1_ready, 1)
                dve.wait_ge(rstd1_ready, u + 1)
                if not (type(u) is int and u == 0):
                    dve.wait_ge(xn1_turned, u)
                for j in range(TJ):
                    last = nc.vector.tensor_scalar(xn1[:, j, :], xin[par][:, j, :], mv1[:, j, 0:1], rstd1[:, j:j + 1],
                                                   ALU.subtract, ALU.mult)
                last.then_inc(xn1_ready, 1)

            def add_x1(v, par):
                dve.wait_ge(relu_turned, v + 1)
                if not (type(v) is int and v == 0):
                    dve.wait_ge(scattered, v * (16 * TJ))
                    dve.wait_ge(x1_stored, v * 16)
                nc.vector.tensor_tensor(pay[:, :, 0:D], ps_r[:], xin[par][:], ALU.add).then_inc(x1_ready, 1)

            def stats_2(v):
                dve.wait_ge(x1_ready, v + 1)
                for j in range(TJ):
                    last = nc.vector.bn_stats(st2[:, j, :], pay[:, j, 0:D])
                last.then_inc(st2_ready, 1)
                wait_alone(dve, st2_ready, v + 1)
                for j in range(TJ):
                    last = nc.vector.bn_aggr(mv2[:, j, :], st2[:, j, :])
                last.then_inc(mv2_ready, 1)

            def norm_2(v):
                dve.wait_ge(std2_ready, v + 1)
                nc.vector.tensor_copy(pay[:, :, MEAN], mv2[:, :, 0])
                nc.vector.reciprocal(pay[:, :, RSTD], std2[:]).then_inc(rstd2_ready, 1)
                dve.wait_ge(rstd2_ready, v + 1)
                if not (type(v) is int and v == 0):
                    dve.wait_ge(xn2_turned, v)
                for j in range(TJ):
                    last = nc.vector.tensor_scalar(xn2[:, j, :], pay[:, j, 0:D], mv2[:, j, 0:1], pay[:, j, RSTD:RSTD + 1],
                                                   ALU.subtract, ALU.mult)
                last.then_inc(xn2_ready, 1)

            def wide(a):
                return a.unsqueeze(2).to_broadcast([TP, TJ, E])

            steps = [0]

            def step(v, instruction):
                steps[0] += 1
                instruction.then_inc(route, 1)
                dve.wait_ge(route, v * ROUTE_STEPS + steps[0])

            def gate_shift(v):
                steps[0] = 0
                dve.wait_ge(logits_made, v + 1)
                gateb = wgt[0:TP, GATEB:GATEB + TJ * E].rearrange("p (j e) -> p j e", e=E)
                step(v, nc.vector.tensor_tensor(logit[:], ps_l[:, 0:TJ * E].rearrange("p (j e) -> p j e", e=E), gateb, ALU.add))
                step(v, nc.vector.reduce_max(lmax[:], logit[:], AX))
                nc.vector.tensor_tensor(logit[:], logit[:], wide(lmax[:]), ALU.subtract).then_inc(shifted_ready, 1)

            def softmax(v):
                dve.wait_ge(exp_ready, v + 1)
                step(v, nc.vector.reduce_sum(esum[:], ex[:], AX))
                step(v, nc.vector.reciprocal(rsum[:], esum[:]))
                step(v, nc.vector.tensor_tensor(prob[:], ex[:], wide(rsum[:]), ALU.mult))
                step(v, nc.vector.reduce_max(pay[:, :, PROB], prob[:], AX))

            def choose(v):
                step(v, nc.vector.tensor_tensor(cand[:], prob[:], wide(pay[:, :, PROB]), ALU.is_equal))
                step(v, nc.vector.tensor_tensor(cand[:], cand[:], cst[0:TP, REV:REV + TJ * E].rearrange("p (j e) -> p j e", e=E), ALU.mult))
                step(v, nc.vector.reduce_max(cmax[:], cand[:], AX))

            def count_rows(v):
                step(v, nc.vector.tensor_tensor(onehot[:], cand[:], wide(cmax[:]), ALU.is_equal))
                nc.vector.reduce_sum(rowsum[:], onehot[:].rearrange("p j e -> p e j"), AX).then_inc(rowsum_ready, 1)

            def place(v):
                dve.wait_ge(counts_made, v + 1)
                step(v, nc.vector.tensor_tensor(before[:, 0, :], ps_l[:, 32:32 + E], carry[:], ALU.add))
                for j in range(1, TJ):
                    step(v, nc.vector.tensor_tensor(before[:, j, :], before[:, j - 1, :], onehot[:, j - 1, :], ALU.add))

            def address(v):
                nc.vector.tensor_tensor(carry[:], carry[:], ps_l[:, 40:40 + E], ALU.add)
                nc.vector.tensor_scalar(over[:], before[:], float(C), float(NOWHERE), ALU.is_ge, ALU.mult)
                step(v, nc.vector.tensor_tensor(where[:], before[:], cst[0:TP, EOFF:EOFF + TJ * E].rearrange("p (j e) -> p j e", e=E), ALU.add))
                step(v, nc.vector.tensor_tensor(where[:], where[:], over[:], ALU.add))

            def slots_of(v):
                nc.vector.tensor_copy(pay_i[:, :, TOKEN], tok[:])
                nc.vector.tensor_scalar(tok[:], tok[:], float(U), None, ALU.add)
                nc.vector.tensor_tensor(where[:], where[:], onehot[:], ALU.mult).then_inc(placed, 1)
                dve.wait_ge(placed, v + 1)
                nc.vector.reduce_max(most[:], carry[:], AX)
                nc.vector.reduce_sum(slot[:], where[:], AX).then_inc(summed, 1)
                dve.wait_ge(summed, v + 1)
                nc.vector.tensor_copy(slot_i[:], slot[:]).then_inc(slots_ready, 1)
                nc.vector.tensor_copy(most_i[:], most[:]).then_inc(most_ready, 1)
                assert steps[0] == ROUTE_STEPS, steps[0]

            def body(u, par):
                first = type(u) is int and u == 0
                for c in range(CHUNKS):
                    split_low(u, c)
                    if first and c + 1 < CHUNKS:
                        h_low(c + 1)
                    if c == 2:
                        stats_1(u, par)
                    if c == 17:
                        norm_1(u, par)
                    if not first:
                        if c == 8:
                            add_x1(u - 1, 1 - par)
                        if c == 10:
                            stats_2(u - 1)
                        if c == 15:
                            norm_2(u - 1)
                        if c == 24:
                            gate_shift(u - 1)
                        if c == 27:
                            softmax(u - 1)
                        if c == 28:
                            choose(u - 1)
                        if c == 29:
                            count_rows(u - 1)
                        if c == 32:
                            place(u - 1)
                        if c == 33:
                            address(u - 1)
                        if c == 34:
                            slots_of(u - 1)

            h_low(0)
            blocks(dve, body)
            add_x1(NB - 1, 1)
            stats_2(NB - 1)
            norm_2(NB - 1)
            gate_shift(NB - 1)
            softmax(NB - 1)
            choose(NB - 1)
            count_rows(NB - 1)
            place(NB - 1)
            address(NB - 1)
            slots_of(NB - 1)

        @block.tensor
        def _(pe):
            def make_h(c):
                if c < FULL:
                    pe.wait_ge(itm_full[c % 4], (c // 4 + 1) * 16)
                if c >= 2:
                    pe.wait_ge(hlo_ready, c - 1)
                for k in range(tiles(c)):
                    rows = P if c < FULL else REST
                    items = itm[c % 4][:, k * P:(k + 1) * P] if c < FULL else wgt[:, ITREST:ITREST + REST]
                    o = ps_h[c % 2][0:rows, k * D:(k + 1) * D]
                    nc.tensor.matmul(o, items, wgt[:, WIT:WIT + D], start=True, stop=False)
                    last = nc.tensor.matmul(o, cst[:, ONES:ONES + rows], wgt[:, BITEM:BITEM + D], start=False, stop=True)
                last.then_inc(h_made, 1)

            def products(u, par, c):
                if type(u) is int and u == 0:
                    pe.wait_ge(hlo_ready, c + 1)
                pe.wait_ge(lo_ready, u * CHUNKS + (c + 1))
                if c == 0 and not (type(u) is int and u < 2):
                    pe.wait_ge(relu_ready, u - 1)
                for k in range(tiles(c)):
                    t = c * CT + k
                    hi, lo = a_hi[c % SPLIT][:, k * U:(k + 1) * U], a_lo[c % SPLIT][:, k * U:(k + 1) * U]
                    wh, wl = h_hi[:, t * D:(t + 1) * D], h_lo[:, t * D:(t + 1) * D]
                    nc.tensor.matmul(acc[par][:], wh, hi, start=(t == 0), stop=False)
                    nc.tensor.matmul(acc[par][:], wh, lo, start=False, stop=False)
                    last = nc.tensor.matmul(acc[par][:], wl, hi, start=False, stop=(t == KT))
                last.then_inc(chunk_done, 1)

            def user_part(u, par):
                pe.wait_ge(xn1t_ready, u + 1)
                nc.tensor.matmul(acc[par][:], wgt[:, WUT:WUT + D], xn1t[:], start=False, stop=False).then_inc(user_added, 1)

            def turn_xn1(u):
                pe.wait_ge(xn1_ready, u + 1)
                for j in range(TJ):
                    last = nc.tensor.transpose(ps_x1[:, j * TP:(j + 1) * TP], xn1[:, j, :], ident[0:TP, 0:TP])
                last.then_inc(xn1_turned, 1)

            def turn_relu(v):
                pe.wait_ge(relu_ready, v + 1)
                for j in range(TJ):
                    last = nc.tensor.transpose(ps_r[:, j, :], rt[:, j * TP:(j + 1) * TP], ident)
                last.then_inc(relu_turned, 1)

            def turn_xn2(v):
                pe.wait_ge(xn2_ready, v + 1)
                for j in range(TJ):
                    last = nc.tensor.transpose(ps_x2[:, j * TP:(j + 1) * TP], xn2[:, j, :], ident[0:TP, 0:TP])
                last.then_inc(xn2_turned, 1)

            def logits(v):
                pe.wait_ge(xn2t_ready, v + 1)
                for j in range(TJ):
                    last = nc.tensor.matmul(ps_l[:, j * E:(j + 1) * E], xn2t[:, j * TP:(j + 1) * TP], wgt[:, GATEW:GATEW + E],
                                            start=True, stop=True)
                last.then_inc(logits_made, 1)

            def count(v):
                pe.wait_ge(rowsum_ready, v + 1)
                nc.tensor.matmul(ps_l[:, 32:32 + E], cst[0:TP, TRI:TRI + TP], rowsum[:], start=True, stop=True)
                nc.tensor.matmul(ps_l[:, 40:40 + E], cst[0:TP, ONES:ONES + TP], rowsum[:], start=True, stop=True).then_inc(counts_made, 1)

            def body(u, par):
                first = type(u) is int and u == 0
                for c in range(CHUNKS):
                    if first and c + AHEAD < CHUNKS:
                        make_h(c + AHEAD)
                    products(u, par, c)
                    if c == 19:
                        turn_xn1(u)
                    if c == 26:
                        user_part(u, par)
                    if not first:
                        if c == 5:
                            turn_relu(u - 1)
                        if c == 17:
                            turn_xn2(u - 1)
                        if c == 21:
                            logits(u - 1)
                        if c == 30:
                            count(u - 1)
            pe.wait_ge(consts_in, 32)
            make_h(0)
            make_h(1)
            blocks(pe, body)
            turn_relu(NB - 1)
            turn_xn2(NB - 1)
            logits(NB - 1)
            count(NB - 1)

        @block.gpsimd
        def _(pool):
            def scatter(v):
                wait_alone(pool, slots_ready, v + 1)
                for j in range(TJ):
                    nc.gpsimd.indirect_dma_start(slots, bass.IndirectOffsetOnAxis(ap=slot_i[:, j:j + 1], axis=0),
                                                 pay[:, j, :], None, bounds_check=E * CP - 1,
                                                 oob_is_err=False).then_inc(scattered, 16)

            pool.wait_ge(filled, 16 * E)
            with pool.Fori(0, NB) as v:
                scatter(v)
            pool.wait_ge(scattered, 16 * TJ * NB)

    def experts(ctx, cst, wgt):
        def sb(name, shape, dt=f32):
            return ctx.enter_context(nc.sbuf_tensor(name, shape, dt))

        def pb(name, shape):
            return ctx.enter_context(nc.psum_tensor(name, shape, f32))

        def sem(name):
            return ctx.enter_context(nc.semaphore(name))

        GC = max(GROUPS) * ROWS
        w1r = [w1r_0, sb("w1r1", [P, F])]
        w2r = [w2r_0, sb("w2r1", [P, FC, D])]
        w1h = [sb(f"w1h{i}", [P, F], f32r) for i in range(2)]
        w1l = [sb(f"w1l{i}", [P, F], f32r) for i in range(2)]
        w2h = [sb(f"w2h{i}", [P, FC, D], f32r) for i in range(2)]
        w2l = [sb(f"w2l{i}", [P, FC, D], f32r) for i in range(2)]
        natx = [sb(f"natx{i}", [ROWS, BLOCKS, W]) for i in range(2)]
        natr = [sb(f"natr{i}", [ROWS, BLOCKS, W]) for i in range(2)]
        xs = [sb(f"xs{i}", [ROWS, BLOCKS, D]) for i in range(2)]
        xh = [sb(f"xh{i}", [P, CP], f32r) for i in range(2)]
        xl = [sb(f"xl{i}", [P, CP], f32r) for i in range(2)]
        hr = [sb(f"hr{i}", [P, FC, GC]) for i in range(2)]
        hh = [sb(f"hh{i}", [P, FC, n * ROWS], f32r) for i, n in enumerate(GROUPS)]
        hl = [sb(f"hl{i}", [P, FC, n * ROWS], f32r) for i, n in enumerate(GROUPS)]
        yt = [sb(f"yt{i}", [P, GC]) for i in range(2)]
        shift = [sb(f"shift{i}", [ROWS, BLOCKS]) for i in range(2)]
        ysum = sb("ysum", [P, E * G])
        yzero = sb("yzero", [P, E * G])
        ybad = sb("ybad", [P, E * G])
        ybads = sb("ybads", [P, 1])
        res = [sb(f"res{i}", [ROWS, n, D]) for i, n in enumerate(GROUPS)]

        ps_1 = [pb(f"ps_1{i}", [P, GC]) for i in range(FC)]
        ps_x = pb("ps_x", [P, GC])
        ps_y = pb("ps_y", [P, GC])
        ps_o = [pb(f"ps_o{i}", [ROWS, 4, D]) for i in range(2)]

        w_full = [sem(f"w_full{i}") for i in range(2)]
        natx_full = [sem(f"natx_full{i}") for i in range(2)]
        natx_first = sem("natx_first")
        natr_full = [sem(f"natr_full{i}") for i in range(2)]
        whi_ready, wlo_ready, xs_ready, x_turned = sem("whi_ready"), sem("wlo_ready"), sem("xs_ready"), sem("x_turned")
        xh_ready, xl_ready, up_made, relu_done = sem("xh_ready"), sem("xl_ready"), sem("up_made"), sem("relu_done")
        hh_ready, hl_ready, down_made, yt_ready = sem("hh_ready"), sem("hl_ready"), sem("down_made"), sem("yt_ready")
        y_turned, res_ready, shift_ready = sem("y_turned"), sem("res_ready"), sem("shift_ready")
        y_stored = [sem(f"y_stored{i}") for i in range(2)]
        flagging, bad_counted = sem("flagging"), sem("bad_counted")
        written = [sem(f"written{i}") for i in range(G)]
        ident = cst[:, IDENT:IDENT + P]

        def each(e, body):
            body(0, 0)
            with e.Fori(0, (E - 2) // 2) as i:
                body(i * 2 + 1, 1)
                body(i * 2 + 2, 0)
            body(E - 1, 1)

        def at(n, least):
            return not (type(n) is int and n < least)

        def of(e, par):
            return (e // 2 + 1) * 16 if type(e) is int else (e + (2 - par)) * 8

        def cols(g):
            return GFIRST[g] * ROWS, GROUPS[g] * ROWS

        def ahead(e, q, g, lead, do):
            if g + lead < G:
                do(e, q, g + lead)
            elif not (type(e) is int and e == E - 1):
                do(e + 1, 1 - q, g + lead - G)

        def behind(e, q, g, lag, do):
            if g >= lag:
                do(e, q, g - lag)
            elif not (type(e) is int and e == 0):
                do(e - 1, 1 - q, g - lag + G)

        def finish(e, q, g, do):
            if type(e) is int and e == E - 1 and g > 0:
                if g == 1:
                    do(e - 1, 1 - q, G - 2)
                    do(e - 1, 1 - q, G - 1)
                else:
                    do(e, q, g - DOWN_LAG)
            else:
                behind(e, q, g, DOWN_LAG + 1, do)

        block = ctx.enter_context(nc.Block())

        @block.sync
        def _(sp):
            def load_w(e, q):
                if at(e, 2):
                    sp.wait_ge(wlo_ready, e - 1)
                sp.dma_start(w1r[q][:], w1[e]).then_inc(w_full[q], 16)
                sp.dma_start(w2r[q][:], w2[e].rearrange("(f p) d -> p f d", p=P)).then_inc(w_full[q], 16)

            def load_x(e, q):
                if at(e, 2):
                    sp.wait_ge(xs_ready, e * G - G)
                sp.dma_start(natx[q][:], slots_v[e]).then_inc(natx_full[q], 16)

            def load_r(e, q):
                if at(e, 2):
                    for g in range(G):
                        wait_alone(sp, written[g], (e - 1) * (16 * GROUPS[g]))
                sp.dma_start(natr[q][:], slots_v[e]).then_inc(natr_full[q], 16)

            def store_y(e, q, g):
                c0, n = cols(g)
                sp.wait_ge(yt_ready, e * G + (g + 1))
                sp.dma_start(y_all[e, :, c0:c0 + n], yt[g % 2][:, 0:n]).then_inc(y_stored[g % 2], 16)

            def body(e, q):
                if not (type(e) is int and e == E - 1):
                    load_x(e + 1, 1 - q)
                    load_w(e + 1, 1 - q)
                for g in range(G):
                    behind(e, q, g, STORE_LAG, store_y)
                    if g == 1:
                        load_r(e, q)

            sp.dma_start(natx[0][:, 0:GROUPS[0], :], slots_v[0, :, 0:GROUPS[0], :]).then_inc(natx_first, 16)
            sp.dma_start(natx[0][:, GROUPS[0]:, :], slots_v[0, :, GROUPS[0]:, :]).then_inc(natx_full[0], 16)
            each(sp, body)
            for g in range(G - STORE_LAG, G):
                store_y(E - 1, 1, g)
            for b in range(2):
                sp.wait_ge(y_stored[b], 16 * E * G // 2)

        @block.scalar
        def _(act):
            def w_high(e, q):
                if not (type(e) is int and e == 0):
                    act.wait_ge(w_full[q], of(e, q) * 2 - (1 - q) * 32)
                if at(e, 2):
                    act.wait_ge(down_made, e * G - G)
                nc.scalar.activation(w1h[q][:], w1r[q][:], ACT.Copy)
                nc.scalar.activation(w2h[q][:], w2r[q][:], ACT.Copy).then_inc(whi_ready, 1)

            def x_high(e, q, g):
                c0, n = cols(g)
                act.wait_ge(x_turned, e * G + (g + 1))
                if at(e, 2):
                    act.wait_ge(up_made, e * (G * FC) - G * FC)
                nc.scalar.activation(xh[q][:, c0:c0 + n], ps_x[:, 0:n], ACT.Copy).then_inc(xh_ready, 1)

            def relu(e, q, g):
                _, n = cols(g)
                if not (type(e) is int and e == 0 and g < 2):
                    act.wait_ge(hl_ready, e * G + (g - 1))
                for f in range(FC):
                    wait_alone(act, up_made, e * (G * FC) + (g * FC + f + 1))
                    nc.scalar.activation(hr[g % 2][:, f, 0:n], ps_1[f][:, 0:n], ACT.Relu,
                                         bias=b1_of(e, f)).then_inc(relu_done, 1)

            def y_out(e, q, g):
                _, n = cols(g)
                wait_alone(act, down_made, e * G + (g + 1))
                if not (type(e) is int and e == 0 and g < 2):
                    wait_alone(act, y_turned, e * G + (g - 1))
                    wait_alone(act, y_stored[g % 2], (e * 2 + g // 2) * 16)
                nc.scalar.activation(yt[g % 2][:, 0:n], ps_y[:, 0:n], ACT.Identity,
                                     bias=b2_of(e), accum_out=sum_of(e, g)).then_inc(yt_ready, 1)

            def b1_of(e, f):
                o = e * FC + (B1 + f)
                return wgt[:, o:o + 1] if type(e) is int else wgt[:, bass.ds(o, 1)]

            def sum_of(e, g):
                o = e * G + g
                return ysum[:, o:o + 1] if type(e) is int else ysum[:, bass.ds(o, 1)]

            def normalise(e, q, g):
                if type(e) is int and e == 0 and g < 2:
                    act.wait_ge(shift_ready, g + 1)
                if g == 0 and at(e, 1):
                    act.wait_ge(shift_ready, e + 2)
                    if at(e, 2):
                        act.wait_ge(x_turned, e * G - G)
                for k in range(GFIRST[g], GFIRST[g] + GROUPS[g]):
                    last = nc.scalar.activation(xs[q][:, k, :], natx[q][:, k, 0:D], ACT.Identity,
                                                scale=natx[q][:, k, RSTD:RSTD + 1], bias=shift[q][:, k:k + 1])
                last.then_inc(xs_ready, 1)

            def b2_of(e):
                o = e + B2
                return wgt[:, o:o + 1] if type(e) is int else wgt[:, bass.ds(o, 1)]

            def body(e, q):
                for g in range(G):
                    relu(e, q, g)
                    ahead(e, q, g, LEAD, x_high)
                    ahead(e, q, g, LEAD + 1, normalise)
                    behind(e, q, g, DOWN_LAG, y_out)
                    if g == 1 and not (type(e) is int and e == E - 1):
                        w_high(e + 1, 1 - q)

            w_high(0, 0)
            for g in range(LEAD):
                normalise(0, 0, g)
            for g in range(LEAD):
                x_high(0, 0, g)
            normalise(0, 0, LEAD)
            each(act, body)
            for g in range(G - DOWN_LAG, G):
                y_out(E - 1, 1, g)

        @block.vector
        def _(dve):
            def w_low(e, q):
                dve.wait_ge(whi_ready, e + 1)
                nc.vector.tensor_tensor(w1l[q][:], w1r[q][:], w1h[q][:].bitcast(f32), ALU.subtract)
                nc.vector.tensor_tensor(w2l[q][:], w2r[q][:], w2h[q][:].bitcast(f32), ALU.subtract).then_inc(wlo_ready, 1)

            def x_low(e, q, g):
                c0, n = cols(g)
                dve.wait_ge(xh_ready, e * G + (g + 1))
                nc.vector.tensor_tensor(xl[q][:, c0:c0 + n], ps_x[:, 0:n], xh[q][:, c0:c0 + n].bitcast(f32),
                                        ALU.subtract).then_inc(xl_ready, 1)

            def split_h(e, g):
                _, n = cols(g)
                b = g % 2
                dve.wait_ge(relu_done, e * (G * FC) + (g + 1) * FC)
                if at(e, 1):
                    dve.wait_ge(down_made, e * G + (g + 1 - G))
                nc.vector.tensor_copy(hh[g][:], hr[b][:, :, 0:n]).then_inc(hh_ready, 1)
                dve.wait_ge(hh_ready, e * G + (g + 1))
                nc.vector.tensor_tensor(hl[g][:], hr[b][:, :, 0:n], hh[g][:].bitcast(f32),
                                        ALU.subtract).then_inc(hl_ready, 1)

            def shifts(e, q):
                dve.wait_ge(natx_full[q], of(e, q))
                if at(e, 2):
                    dve.wait_ge(xs_ready, e * G - G)
                shifts_of(q, 0, BLOCKS)

            def shifts_of(q, b0, b1):
                nc.vector.scalar_tensor_tensor(out=shift[q][:, b0:b1], in0=natx[q][:, b0:b1, MEAN], scalar=-1.0,
                                               in1=natx[q][:, b0:b1, RSTD], op0=ALU.mult, op1=ALU.mult).then_inc(shift_ready, 1)

            def result(e, q, g):
                b = g % 2
                if g == 0:
                    dve.wait_ge(natr_full[q], of(e, q))
                dve.wait_ge(y_turned, e * G + (g + 1))
                if at(e, 1):
                    dve.wait_ge(written[g], e * (16 * GROUPS[g]))
                for k in range(GROUPS[g]):
                    row = natr[q][:, GFIRST[g] + k, :]
                    last = nc.vector.scalar_tensor_tensor(out=res[g][:, k, :], in0=ps_o[b][:, k, :], scalar=row[:, PROB:PROB + 1],
                                                          in1=row[:, 0:D], op0=ALU.mult, op1=ALU.add)
                last.then_inc(res_ready, 1)

            def body(e, q):
                others = not (type(e) is int and e == E - 1)
                for g in range(G):
                    ahead(e, q, g, LEAD, x_low)
                    if g == 0 and others:
                        shifts(e + 1, 1 - q)
                    if g == 2 and others:
                        w_low(e + 1, 1 - q)
                    soon = type(e) is int and e == E - 1 and g > 1
                    if soon:
                        finish(e, q, g, result)
                    split_h(e, g)
                    if not soon:
                        finish(e, q, g, result)

            w_low(0, 0)
            dve.wait_ge(natx_first, 16)
            shifts_of(0, 0, GROUPS[0])
            dve.wait_ge(natx_full[0], 16)
            shifts_of(0, GROUPS[0], BLOCKS)
            for g in range(LEAD):
                x_low(0, 0, g)
            each(dve, body)
            for g in range(G - DOWN_LAG, G):
                result(E - 1, 1, g)
            dve.wait_ge(yt_ready, E * G)
            nc.vector.tensor_scalar(yzero[:], ysum[:], 0.0, None, ALU.mult).then_inc(flagging, 1)
            dve.wait_ge(flagging, 1)
            nc.vector.tensor_scalar(ybad[:], yzero[:], 0.0, None, ALU.not_equal).then_inc(flagging, 1)
            dve.wait_ge(flagging, 2)
            nc.vector.reduce_sum(ybads[:], ybad[:], AX).then_inc(flagging, 1)
            dve.wait_ge(bad_counted, 1)
            nc.vector.tensor_copy(not_finite[:], ps_x[0:1, 0:1]).then_inc(flagging, 1)

        @block.tensor
        def _(pe):
            def turn_x(e, q, g):
                pe.wait_ge(xs_ready, e * G + (g + 1))
                if not (type(e) is int and e == 0 and g == 0):
                    pe.wait_ge(xl_ready, e * G + g)
                for k in range(GROUPS[g]):
                    last = nc.tensor.transpose(ps_x[:, k * ROWS:(k + 1) * ROWS], xs[q][:, GFIRST[g] + k, :],
                                               ident[0:ROWS, 0:ROWS])
                last.then_inc(x_turned, 1)

            def up(e, q, g):
                c0, n = cols(g)
                if g == 0:
                    pe.wait_ge(wlo_ready, e + 1)
                pe.wait_ge(xl_ready, e * G + (g + 1))
                for f in range(FC):
                    if not (type(e) is int and e == 0 and g == 0):
                        pe.wait_ge(relu_done, e * (G * FC) + ((g - 1) * FC + f + 1))
                    wh, wl = w1h[q][:, f * P:(f + 1) * P], w1l[q][:, f * P:(f + 1) * P]
                    o = ps_1[f][:, 0:n]
                    nc.tensor.matmul(o, wh, xh[q][:, c0:c0 + n], start=True, stop=False)
                    nc.tensor.matmul(o, wh, xl[q][:, c0:c0 + n], start=False, stop=False)
                    nc.tensor.matmul(o, wl, xh[q][:, c0:c0 + n], start=False, stop=True).then_inc(up_made, 1)

            def down(e, q, g):
                _, n = cols(g)
                pe.wait_ge(hl_ready, e * G + (g + 1))
                if not (type(e) is int and e == 0 and g == 0):
                    pe.wait_ge(yt_ready, e * G + g)
                for f in range(FC):
                    o = ps_y[:, 0:n]
                    hi, lo = hh[g][:, f, :], hl[g][:, f, :]
                    nc.tensor.matmul(o, w2h[q][:, f, :], hi, start=(f == 0), stop=False)
                    nc.tensor.matmul(o, w2h[q][:, f, :], lo, start=False, stop=False)
                    last = nc.tensor.matmul(o, w2l[q][:, f, :], hi, start=False, stop=(f == FC - 1))
                last.then_inc(down_made, 1)

            def turn_y(e, q, g):
                b = g % 2
                pe.wait_ge(yt_ready, e * G + (g + 1))
                if not (type(e) is int and e == 0 and g < 2):
                    pe.wait_ge(res_ready, e * G + (g - 1))
                for k in range(GROUPS[g]):
                    last = nc.tensor.transpose(ps_o[b][:, k, :], yt[b][:, k * ROWS:(k + 1) * ROWS], ident)
                last.then_inc(y_turned, 1)

            def body(e, q):
                for g in range(G):
                    up(e, q, g)
                    ahead(e, q, g, LEAD, turn_x)
                    behind(e, q, g, DOWN_LAG, down)
                    finish(e, q, g, turn_y)

            for g in range(LEAD):
                turn_x(0, 0, g)
            each(pe, body)
            for g in range(G - DOWN_LAG, G):
                down(E - 1, 1, g)
                turn_y(E - 1, 1, g)
            pe.wait_ge(flagging, 3)
            nc.tensor.matmul(ps_x[0:1, 0:1], ybads[:], cst[:, ONES:ONES + 1], start=True, stop=True).then_inc(bad_counted, 1)

        @block.gpsimd
        def _(pool):
            def write(e, q, g):
                wait_alone(pool, res_ready, e * G + (g + 1))
                for k in range(GROUPS[g]):
                    token = natr[q][:].bitcast(i32)[:, GFIRST[g] + k, TOKEN:TOKEN + 1]
                    nc.gpsimd.indirect_dma_start(out, bass.IndirectOffsetOnAxis(ap=token, axis=0), res[g][:, k, :], None,
                                                 bounds_check=T - 1, oob_is_err=False).then_inc(written[g], 16)

            def body(e, q):
                for g in range(G):
                    finish(e, q, g, write)

            each(pool, body)
            for g in range(G - DOWN_LAG, G):
                write(E - 1, 1, g)
            for g in range(G):
                pool.wait_ge(written[g], E * 16 * GROUPS[g])

    def guard(ctx, cst):
        def sb(name, shape, dt=f32):
            return ctx.enter_context(nc.sbuf_tensor(name, shape, dt))

        yb = sb("yb", [P, ROWS])
        row = sb("row", [ROWS, W])
        y = sb("y", [ROWS, D])
        above = sb("above", [ROWS, D])
        below = sb("below", [ROWS, D])
        less = sb("less", [ROWS, D])
        finite = sb("finite", [ROWS, D], i32)
        fixed = sb("fixed", [ROWS, D])
        ps = ctx.enter_context(nc.psum_tensor("ps", [ROWS, D], f32))
        loaded, turned, guarding, rewritten, block_free = [
            ctx.enter_context(nc.semaphore(n)) for n in ("loaded", "turned", "guarding", "rewritten", "block_free")]
        STEPS = 5

        def every(engine, body):
            flag = engine.value_load(not_finite[0:1, 0:1])
            with engine.If(flag > 0):
                with engine.Fori(0, E) as e:
                    with engine.Fori(0, BLOCKS) as b:
                        body(e, b, e * BLOCKS + (b + 1))

        block = ctx.enter_context(nc.Block())

        @block.sync
        def _(sp):
            def body(e, b, k):
                sp.wait_ge(block_free, k)
                sp.dma_start(yb[:], y_all[e, :, bass.ds(b * ROWS, ROWS)]).then_inc(loaded, 16)
                sp.dma_start(row[:], slots_b[e, b]).then_inc(loaded, 16)
            every(sp, body)

        @block.tensor
        def _(pe):
            def body(e, b, k):
                pe.wait_ge(loaded, k * 32)
                nc.tensor.transpose(ps[:], yb[:], cst[:, IDENT:IDENT + P]).then_inc(turned, 1)
            every(pe, body)

        @block.vector
        def _(dve):
            def body(e, b, k):
                def step(i, instruction):
                    instruction.then_inc(guarding, 1)
                    wait_alone(dve, guarding, k * STEPS + (i - STEPS))

                wait_alone(dve, turned, k)
                step(1, nc.vector.tensor_scalar(y[:], ps[:], row[:, PROB:PROB + 1], None, ALU.mult))
                nc.vector.tensor_scalar(above[:], y[:], 0.0, 1e4, ALU.is_gt, ALU.mult)
                nc.vector.tensor_scalar(below[:], y[:], 0.0, 1e4, ALU.is_lt, ALU.mult)
                step(2, nc.vector.tensor_tensor(less[:], y[:], y[:], ALU.subtract))
                nc.vector.tensor_scalar(finite[:], less[:], 0.0, None, ALU.is_equal)
                step(3, nc.vector.tensor_tensor(fixed[:], above[:], below[:], ALU.subtract))
                step(4, nc.vector.copy_predicated(fixed[:], finite[:], y[:]))
                step(5, nc.vector.tensor_tensor(fixed[:], fixed[:], row[:, 0:D], ALU.add))
            every(dve, body)

        @block.gpsimd
        def _(pool):
            pool.sem_inc(block_free, 1)

            def body(e, b, k):
                wait_alone(pool, guarding, k * STEPS)
                nc.gpsimd.indirect_dma_start(out, bass.IndirectOffsetOnAxis(ap=row[:].bitcast(i32)[:, TOKEN:TOKEN + 1], axis=0),
                                             fixed[:], None, bounds_check=T - 1, oob_is_err=False).then_inc(rewritten, 16)
                wait_alone(pool, rewritten, k * 16)
                pool.sem_inc(block_free, 1)
            every(pool, body)

    with ExitStack() as ctx:
        not_finite = ctx.enter_context(nc.sbuf_tensor("not_finite", [1, 1], i32))
        consts_in = ctx.enter_context(nc.semaphore("consts_in"))
        w1r_0 = ctx.enter_context(nc.sbuf_tensor("w1r0", [P, F], f32))
        w2r_0 = ctx.enter_context(nc.sbuf_tensor("w2r0", [P, FC, D], f32))
        w_first = ctx.enter_context(nc.semaphore("w_first"))
        cst = ctx.enter_context(nc.sbuf_tensor("cst", [P, CONST_W], f32))
        wgt = ctx.enter_context(nc.sbuf_tensor("wgt", [P, WEIGHT_W], f32))
        with ExitStack() as inner:
            stream(inner, cst, wgt)
        with ExitStack() as inner:
            experts(inner, cst, wgt)
        with ExitStack() as inner:
            guard(inner, cst)


def kernel(x, adj, L0_gnn_item_feat, L0_gnn_W_item, L0_gnn_b_item, L0_gnn_W_user, L0_gnn_b_user,
           L0_ffn_gate_w, L0_ffn_gate_b, L0_ffn_w1, L0_ffn_b1, L0_ffn_w2, L0_ffn_b2):
    import numpy as np
    import concourse.bacc as bacc
    from concourse.bass_utils import run_bass_kernel_spmd

    f = np.float32
    a = np.asarray(adj).reshape(NB, TP, TJ, N)
    main = np.empty((NB, KT // PER_ROW, P, PER_ROW, TJ, TP), f)
    for u in range(NB):
        t = np.ascontiguousarray(a[u].transpose(2, 1, 0))
        main[u] = t[:KT * P].reshape(KT // PER_ROW, PER_ROW, P, TJ, TP).transpose(0, 2, 1, 3, 4)
    rest = np.ascontiguousarray(a[:, :, :, KT * P:].transpose(0, 3, 2, 1)).reshape(NB, REST, U)
    item_t = np.ascontiguousarray(np.asarray(L0_gnn_item_feat).T)

    const = np.zeros((P, CONST_W), f)
    const[:, IDENT:IDENT + P] = np.eye(P)
    const[:, TRI:TRI + P] = np.triu(np.ones((P, P)), 1)
    const[:, ONES:ONES + P] = 1.0
    const[:, REV:REV + TJ * E] = np.tile(np.arange(E, 0, -1), TJ)
    const[:, EOFF:EOFF + TJ * E] = np.tile(np.arange(E) * CP, TJ)
    const[:, TOK0:TOK0 + TJ] = np.arange(P)[:, None] * TJ + np.arange(TJ)

    weights = np.zeros((P, WEIGHT_W), f)
    weights[:, WIT:WIT + D] = np.asarray(L0_gnn_W_item).T
    weights[:, WUT:WUT + D] = np.asarray(L0_gnn_W_user).T
    weights[0, BITEM:BITEM + D] = L0_gnn_b_item
    weights[:, ITREST:ITREST + REST] = item_t[:, KT * P:]
    weights[:, GATEW:GATEW + E] = L0_ffn_gate_w
    weights[:, GATEB:GATEB + TJ * E] = np.tile(np.asarray(L0_ffn_gate_b), TJ)
    weights[:, BUSER] = L0_gnn_b_user
    weights[:, B1:B1 + E * FC] = np.asarray(L0_ffn_b1).reshape(E * FC, P).T
    weights[:, B2:B2 + E] = np.asarray(L0_ffn_b2).T

    arrays = {
        "adj_main": main.reshape(NB, KT // PER_ROW, P, PER_ROW * U), "adj_rest": rest, "x_in": np.ascontiguousarray(x),
        "item_t": item_t, "const": const, "weights": weights,
        "w1_in": np.ascontiguousarray(L0_ffn_w1), "w2_in": np.ascontiguousarray(L0_ffn_w2),
    }
    nc = bacc.Bacc("TRN2", target_bir_lowering=False, num_devices=1)
    args = [nc.dram_tensor(k, v.shape, mybir.dt.from_np(v.dtype), kind="ExternalInput").ap() for k, v in arrays.items()]
    out = nc.dram_tensor("out", (T, D), mybir.dt.float32, kind="ExternalOutput").ap()
    build(nc, *args, out)
    return run_bass_kernel_spmd(nc, [arrays], core_ids=[0]).results[0]["out"]
```
